# Optimizing a Trainium2 kernel written in Bass

```python
import numpy as np
import jax
import jax.numpy as jnp

def _softmax(x, axis=-1):
    return jax.nn.softmax(x, axis=axis)

def _gelu(x):
    return jax.nn.gelu(x, approximate=True)

def _silu(x):
    return jax.nn.silu(x)

def _sigmoid(x):
    return jax.nn.sigmoid(x)

def _layernorm(x, axis=-1, eps=1e-05):
    m = jnp.mean(x, axis=axis, keepdims=True)
    v = jnp.var(x, axis=axis, keepdims=True)
    return (x - m) / jnp.sqrt(v + eps)

def _scatter_add(tgt, idx, src, axis=0):
    return tgt.at[idx].add(src)

def _segment_sum(src, seg, n):
    return jax.ops.segment_sum(src, seg, n)
kernel_name = 'mk_gnn_preln_d2_gnn_r32_a7c874'

def setup_inputs(seed: int=0):
    np.random.seed(seed)
    _w = jnp.asarray

    def _rec_inputs():
        import jax
        import jax.numpy as jnp
        _gk = jax.random.key(seed)
        x = -0.0003713 + 1 * jax.random.normal(jax.random.fold_in(_gk, 1), (3125, 128), jnp.float32)
        _s = jax.random.randint(jax.random.fold_in(_gk, 2), (50000,), 0, 3125, jnp.int32)
        _d = jax.random.randint(jax.random.fold_in(_gk, 3), (50000,), 0, 3125, jnp.int32)
        _loop = jnp.arange(3125, dtype=jnp.int32)
        src = jnp.concatenate([_s, _d, _loop])
        dst = jnp.concatenate([_d, _s, _loop])
        _o = jnp.argsort(dst, stable=True)
        src = src[_o]
        dst = dst[_o]
        edge_type_16 = jax.random.randint(jax.random.fold_in(_gk, 12), (103125,), 0, 16, jnp.int32)
        return (x, src, dst, edge_type_16)
    x, src, dst, edge_type_16 = _rec_inputs()

    def _L0_gnn_setup():
        import jax, jax.numpy as jnp
        import numpy as np
        N, E = (3125, 50000)
        IN_DIM, HID, OUT_DIM = (128, 256, 128)
        LN_EPS = 1e-05

        def _gcn_norm(edge_index, n_nodes):
            loops = jnp.arange(n_nodes, dtype=edge_index.dtype)
            src = jnp.concatenate([edge_index[0], loops])
            dst = jnp.concatenate([edge_index[1], loops])
            deg = jax.ops.segment_sum(jnp.ones_like(dst, dtype=jnp.float32), dst, num_segments=n_nodes)
            dinv = jnp.where(deg > 0, jax.lax.rsqrt(deg), 0.0)
            norm = dinv[src] * dinv[dst]
            return (src, dst, norm)

        def _gcn_conv(x, W, b, src, dst, norm, n_nodes):
            h = x @ W
            msg = h[src] * norm[:, None]
            out = jax.ops.segment_sum(msg, dst, num_segments=n_nodes)
            return out + b

        def _layernorm(x, g, b):
            mu = jnp.mean(x, axis=-1, keepdims=True)
            var = jnp.mean(jnp.square(x - mu), axis=-1, keepdims=True)
            return (x - mu) * jax.lax.rsqrt(var + LN_EPS) * g + b
        key = jax.random.key(seed)
        ks = jax.random.split(key, 16)
        inp = {'x': jax.random.normal(ks[0], (N, IN_DIM), dtype=jnp.float32), 'edge_index': jax.random.randint(ks[1], (2, E), 0, N, dtype=jnp.int32), 'W0': jax.random.normal(ks[2], (IN_DIM, HID), dtype=jnp.float32) * 0.05, 'b0': jnp.zeros((HID,), dtype=jnp.float32), 'W1': jax.random.normal(ks[3], (HID, HID), dtype=jnp.float32) * 0.05, 'b1': jnp.zeros((HID,), dtype=jnp.float32), 'W2': jax.random.normal(ks[4], (HID, HID), dtype=jnp.float32) * 0.05, 'b2': jnp.zeros((HID,), dtype=jnp.float32), 'W3': jax.random.normal(ks[5], (HID, OUT_DIM), dtype=jnp.float32) * 0.05, 'b3': jnp.zeros((OUT_DIM,), dtype=jnp.float32), 'a0': jnp.ones((1,), dtype=jnp.float32), 'a1': jnp.ones((1,), dtype=jnp.float32), 'a2': jnp.ones((1,), dtype=jnp.float32), 'g0': jnp.ones((HID,), dtype=jnp.float32), 'beta0': jnp.zeros((HID,), dtype=jnp.float32), 'g1': jnp.ones((HID,), dtype=jnp.float32), 'beta1': jnp.zeros((HID,), dtype=jnp.float32), 'g2': jnp.ones((HID,), dtype=jnp.float32), 'beta2': jnp.zeros((HID,), dtype=jnp.float32)}
        return inp
    _L0_gnn_all = _L0_gnn_setup()
    _L0_gnn_in = {k: v for k, v in _L0_gnn_all.items() if k in ('W0', 'b0', 'W1', 'b1', 'W2', 'b2', 'W3', 'b3', 'a0', 'a1', 'a2', 'g0', 'beta0', 'g1', 'beta1', 'g2', 'beta2')}
    del _L0_gnn_all

    def _L1_gnn_setup():
        import jax, jax.numpy as jnp
        import numpy as np
        NUM_NODES = 50000
        NUM_RELATIONS = 16
        HIDDEN = 128
        NUM_LAYERS = 3
        NUM_EDGES = 50000

        def _fast_rgcn_layer(x, src, tgt, edge_type, W_r, root_r, bias_r):
            N, d = x.shape
            R = W_r.shape[0]
            seg = tgt * R + edge_type
            msg = x[src]
            agg = jax.ops.segment_sum(msg, seg, num_segments=N * R).reshape(N, R, d)
            cnt = jax.ops.segment_sum(jnp.ones_like(edge_type, dtype=x.dtype), seg, num_segments=N * R).reshape(N, R, 1)
            agg = agg / jnp.clip(cnt, 1.0, None)
            out = jnp.einsum('nrd,rdo->no', agg, W_r)
            out = out + x @ root_r + bias_r
            return out
        key = jax.random.key(seed)
        ks = jax.random.split(key, 6)
        edge_index = jax.random.randint(ks[0], (2, NUM_EDGES), 0, NUM_NODES, dtype=jnp.int64)
        edge_type = jax.random.randint(ks[1], (NUM_EDGES,), 0, NUM_RELATIONS, dtype=jnp.int64)
        scale = 1.0 / np.sqrt(HIDDEN)
        node_init = jax.random.normal(ks[2], (NUM_NODES, HIDDEN), dtype=jnp.float32) * scale
        W = jax.random.normal(ks[3], (NUM_LAYERS, NUM_RELATIONS, HIDDEN, HIDDEN), dtype=jnp.float32) * scale
        root = jax.random.normal(ks[4], (NUM_LAYERS, HIDDEN, HIDDEN), dtype=jnp.float32) * scale
        bias = jnp.zeros((NUM_LAYERS, HIDDEN), dtype=jnp.float32)
        return {'edge_index': edge_index, 'edge_type': edge_type, 'node_init': node_init, 'W': W, 'root': root, 'bias': bias}
    _L1_gnn_all = _L1_gnn_setup()
    _L1_gnn_in = {k: v for k, v in _L1_gnn_all.items() if k in ('W', 'root', 'bias')}
    del _L1_gnn_all
    return {'x': x, 'src': src, 'dst': dst, 'edge_type_16': edge_type_16, 'L0_gnn_W0': _L0_gnn_in['W0'], 'L0_gnn_b0': _L0_gnn_in['b0'], 'L0_gnn_W1': _L0_gnn_in['W1'], 'L0_gnn_b1': _L0_gnn_in['b1'], 'L0_gnn_W2': _L0_gnn_in['W2'], 'L0_gnn_b2': _L0_gnn_in['b2'], 'L0_gnn_W3': _L0_gnn_in['W3'], 'L0_gnn_b3': _L0_gnn_in['b3'], 'L0_gnn_a0': _L0_gnn_in['a0'], 'L0_gnn_a1': _L0_gnn_in['a1'], 'L0_gnn_a2': _L0_gnn_in['a2'], 'L0_gnn_g0': _L0_gnn_in['g0'], 'L0_gnn_beta0': _L0_gnn_in['beta0'], 'L0_gnn_g1': _L0_gnn_in['g1'], 'L0_gnn_beta1': _L0_gnn_in['beta1'], 'L0_gnn_g2': _L0_gnn_in['g2'], 'L0_gnn_beta2': _L0_gnn_in['beta2'], 'L1_gnn_W': _L1_gnn_in['W'], 'L1_gnn_root': _L1_gnn_in['root'], 'L1_gnn_bias': _L1_gnn_in['bias']}

def reference(x, src, dst, edge_type_16, L0_gnn_W0, L0_gnn_b0, L0_gnn_W1, L0_gnn_b1, L0_gnn_W2, L0_gnn_b2, L0_gnn_W3, L0_gnn_b3, L0_gnn_a0, L0_gnn_a1, L0_gnn_a2, L0_gnn_g0, L0_gnn_beta0, L0_gnn_g1, L0_gnn_beta1, L0_gnn_g2, L0_gnn_beta2, L1_gnn_W, L1_gnn_root, L1_gnn_bias):
    import jax
    import jax.numpy as jnp

    def _L0_gnn_ref(x, edge_index, W0, b0, W1, b1, W2, b2, W3, b3, a0, a1, a2, g0, beta0, g1, beta1, g2, beta2):
        import jax, jax.numpy as jnp
        import numpy as np
        N, E = (3125, 50000)
        IN_DIM, HID, OUT_DIM = (128, 256, 128)
        LN_EPS = 1e-05

        def _gcn_norm(edge_index, n_nodes):
            loops = jnp.arange(n_nodes, dtype=edge_index.dtype)
            src = jnp.concatenate([edge_index[0], loops])
            dst = jnp.concatenate([edge_index[1], loops])
            deg = jax.ops.segment_sum(jnp.ones_like(dst, dtype=jnp.float32), dst, num_segments=n_nodes)
            dinv = jnp.where(deg > 0, jax.lax.rsqrt(deg), 0.0)
            norm = dinv[src] * dinv[dst]
            return (src, dst, norm)

        def _gcn_conv(x, W, b, src, dst, norm, n_nodes):
            h = x @ W
            msg = h[src] * norm[:, None]
            out = jax.ops.segment_sum(msg, dst, num_segments=n_nodes)
            return out + b

        def _layernorm(x, g, b):
            mu = jnp.mean(x, axis=-1, keepdims=True)
            var = jnp.mean(jnp.square(x - mu), axis=-1, keepdims=True)
            return (x - mu) * jax.lax.rsqrt(var + LN_EPS) * g + b
        n_nodes = x.shape[0]
        src, dst, norm = _gcn_norm(edge_index, n_nodes)
        layers = [(W0, b0, a0, g0, beta0), (W1, b1, a1, g1, beta1), (W2, b2, a2, g2, beta2)]
        h = x
        for W, b, a, g, beta in layers:
            c = _gcn_conv(h, W, b, src, dst, norm, n_nodes)
            c = c * jax.nn.sigmoid(a)
            c = _layernorm(c, g, beta)
            h = jax.nn.elu(c)
        return _gcn_conv(h, W3, b3, src, dst, norm, n_nodes)

    def _L1_gnn_ref(edge_index, edge_type, node_init, W, root, bias):
        import jax, jax.numpy as jnp
        import numpy as np
        NUM_NODES = 50000
        NUM_RELATIONS = 16
        HIDDEN = 128
        NUM_LAYERS = 3
        NUM_EDGES = 50000

        def _fast_rgcn_layer(x, src, tgt, edge_type, W_r, root_r, bias_r):
            N, d = x.shape
            R = W_r.shape[0]
            seg = tgt * R + edge_type
            msg = x[src]
            agg = jax.ops.segment_sum(msg, seg, num_segments=N * R).reshape(N, R, d)
            cnt = jax.ops.segment_sum(jnp.ones_like(edge_type, dtype=x.dtype), seg, num_segments=N * R).reshape(N, R, 1)
            agg = agg / jnp.clip(cnt, 1.0, None)
            out = jnp.einsum('nrd,rdo->no', agg, W_r)
            out = out + x @ root_r + bias_r
            return out
        src, tgt = (edge_index[0], edge_index[1])
        x = node_init
        for i in range(NUM_LAYERS):
            x = _fast_rgcn_layer(x, src, tgt, edge_type, W[i], root[i], bias[i])
            if i < NUM_LAYERS - 1:
                x = jax.nn.relu(x)
        return x
    edge_index = jnp.stack([src, dst])
    h = jnp.maximum(_layernorm(x, axis=-1), 0.0)
    x = x + _L0_gnn_ref(h, edge_index, L0_gnn_W0, L0_gnn_b0, L0_gnn_W1, L0_gnn_b1, L0_gnn_W2, L0_gnn_b2, L0_gnn_W3, L0_gnn_b3, L0_gnn_a0, L0_gnn_a1, L0_gnn_a2, L0_gnn_g0, L0_gnn_beta0, L0_gnn_g1, L0_gnn_beta1, L0_gnn_g2, L0_gnn_beta2)
    h = jnp.maximum(_layernorm(x, axis=-1), 0.0)
    x = x + _L1_gnn_ref(edge_index, edge_type_16, h, L1_gnn_W, L1_gnn_root, L1_gnn_bias)
    return x

_drawn_inputs = setup_inputs


def setup_inputs(seed=0):
    import zlib

    import numpy as np

    out = dict(_drawn_inputs(seed))
    spreads = {'L0_gnn_b0': (0.0, 0.1),
     'L0_gnn_b1': (0.0, 0.1),
     'L0_gnn_b2': (0.0, 0.1),
     'L0_gnn_b3': (0.0, 0.1),
     'L0_gnn_g0': (1.0, 0.2),
     'L0_gnn_beta0': (0.0, 0.1),
     'L0_gnn_g1': (1.0, 0.2),
     'L0_gnn_beta1': (0.0, 0.1),
     'L0_gnn_g2': (1.0, 0.2),
     'L0_gnn_beta2': (0.0, 0.1),
     'L1_gnn_bias': (0.0, 0.1)}
    factors = {}
    for name, (base, spread) in spreads.items():
        noise = np.random.default_rng([zlib.crc32(name.encode()), seed]).standard_normal(out[name].shape)
        drawn = base * np.exp(spread * noise) if base else spread * noise
        out[name] = jnp.asarray(drawn.astype(out[name].dtype))
    for name, factor in factors.items():
        out[name] = (out[name] * factor).astype(out[name].dtype)
    return out
```

```python
import numpy as np
import concourse.bass as bass
from concourse import mybir
from contextlib import ExitStack

F32, F16, I32 = mybir.dt.float32, mybir.dt.float16, mybir.dt.int32
ALU = mybir.AluOpType
ACT = mybir.ActivationFunctionType
AX = mybir.AxisListType

P = 128
NODES, EDGES = 3125, 103125
BLOCKS = -(-NODES // P)
NPAD = BLOCKS * P
WIN = 24
TILES = -(-EDGES // P)
GT = 4
TPAD = 816
GPAD = TPAD // GT
EDGE_TILES = 808
LAST = EDGES - (TILES - 1) * P
IN_F, HID, REL, RF = 128, 256, 16, 128
F16_TOP = 60000.0
SCALE = 16.0
SCALE3 = 4.0
EPS = 1e-5


class Tally:

    def __init__(self, sem):
        self.sem, self.n, self.loop = sem, 0, None

    def inc(self, ins):
        ins.then_inc(self.sem, 1)
        self.n += 1
        return ins

    def enter(self, i, per):
        self.loop = (i, per, self.n)

    def leave(self, iterations):
        i, per, n0 = self.loop
        assert self.n - n0 == per, (self.n - n0, per)
        self.n, self.loop = n0 + per * iterations, None

    def now(self):
        return self.n if self.loop is None else self.loop[0] * self.loop[1] + self.n

    def link(self, eng, ins):
        self.inc(ins)
        eng.wait_ge(self.sem, self.now())
        return ins


class Prog:

    def __init__(self, nc, ctx, dram):
        self.nc, self.ctx, self.d = nc, ctx, dram

        def sb(name, shape, dt):
            return ctx.enter_context(nc.sbuf_tensor(name, shape, dt))

        self.arena = sb("arena", [P, BLOCKS * NPAD], F16)
        self.h16 = sb("h16", [P, BLOCKS, 2, HID], F16)
        self.work = sb("work", [P, 4 * 5 * HID], F32)
        self.wts = sb("wts", [P, 2, HID], F32)
        self.rows = sb("rows", [P, 3, HID], F32)
        self.ident = sb("ident", [P, P], F32)
        self.cols = sb("cols", [P, 4, BLOCKS], F32)
        self.flag = sb("flag", [1, 1], I32)
        self.small = sb("small", [P, 4], F32)
        self.lnbuf = sb("lnbuf", [P, 68], F32)
        self.csig = sb("csig", [P, BLOCKS], F32)
        self.psum = ctx.enter_context(nc.psum_tensor("psum", [P, 8, 512], F32))
        self.n_sem, self.live = 0, []
        self.at = 0

    def sem(self, name):
        self.n_sem += 1
        handle = self.nc.alloc_semaphore(f"{name}_{self.n_sem}")
        self.live.append(handle)
        return handle

    def end_stage(self):
        self.nc.clear_and_free_semaphores(self.live)
        self.nc.all_engine_barrier()
        self.live = []

    def carve(self, start=None):
        if start is not None:
            self.at = start
        whole = self.arena[:, :].bitcast(F32)

        def piece(words, dt=F32, parts=P):
            a = whole[0:parts, self.at:self.at + words]
            self.at += words
            assert self.at <= BLOCKS * NPAD // 2, self.at
            return a if dt == F32 else a.bitcast(dt)
        return piece


class Bodies:

    def __init__(self):
        self.of = {}

    def sync(self, f):
        self.of["sync"] = f

    def gpsimd(self, f):
        self.of["gpsimd"] = f

    def scalar(self, f):
        self.of["scalar"] = f

    def vector(self, f):
        self.of["vector"] = f

    def tensor(self, f):
        self.of["tensor"] = f


def run(p, fast, general=None):

    def body(name):
        def both(e):
            f = fast.of.get(name)
            g = general.of.get(name) if general else None
            if not general:
                f(e)
                return
            asked = e.value_load(p.flag[0:1, 0:1], min_val=0, max_val=1)
            if f:
                with e.If(asked == 0):
                    f(e)
            if g:
                with e.If(asked == 1):
                    g(e)
        return both

    with p.nc.Block() as block:
        at = dict(sync=block.sync, gpsimd=block.gpsimd, scalar=block.scalar, vector=block.vector, tensor=block.tensor)
        for name, decorate in at.items():
            if name in fast.of or (general and name in general.of):
                decorate(body(name))
    p.end_stage()


class Serial:

    def __init__(self, p, steps, iterations):
        self.steps, self.iterations = steps, iterations
        self.done, self.dma, self.passed = p.sem("steps"), p.sem("gathered"), p.sem("passed")

    def body(self, e, me):
        if me == "vector":
            e.sem_inc(self.done)
        per = len(self.steps)
        with e.Fori(0, self.iterations) as i:
            for n, (engine, step) in enumerate(self.steps):
                if engine != me:
                    continue
                held(e, self.done, i * per + n + 1, self.passed)
                ins = step(e, i)
                if engine == "gpsimd":
                    ins.then_inc(self.dma, 16)
                    e.wait_ge(self.dma, i * 16 + 16)
                    e.sem_inc(self.done)
                else:
                    ins.then_inc(self.done, 1)
        e.wait_ge(self.done, self.iterations * per + 1)


def held(eng, sem, value, passed):
    eng.wait_ge(sem, value)
    eng.sem_inc(passed)


def bcast(ap, parts, at, n):
    return ap.rearrange("p (n o) -> p n o", o=1).to_broadcast([parts, n, at])


def prepare(p, t):
    nc, d = p.nc, p.d
    s_ld, s_io, s_ps = p.sem("loaded"), p.sem("iota"), p.sem("summed")
    s_sq = p.sem("sqrt")
    block = Bodies()

    @block.sync
    def _(e):
        e.dma_start(t.src, d["src_pt"][:, :]).then_inc(s_ld, 16)
        e.dma_start(t.dst, d["dst_pt"][:, :]).then_inc(s_ld, 16)
        e.dma_start(t.typ, d["typ_pt"][:, :]).then_inc(s_ld, 16)
        e.dma_start(t.gbase, d["gbase"].partition_broadcast(P)).then_inc(s_ld, 16)
        for k in range(3):
            e.dma_start(t.gains[:, k], d[f"g{k}"].partition_broadcast(P)).then_inc(s_ld, 16)
            e.dma_start(t.gains[:, 3 + k], d[f"beta{k}"].partition_broadcast(P)).then_inc(s_ld, 16)
            e.dma_start(t.sig[:, k:k + 1], d[f"a{k}"].partition_broadcast(P)).then_inc(s_ld, 16)
        e.wait_ge(s_ld, 13 * 16)

    @block.gpsimd
    def _(e):
        big = dict(allow_small_or_imprecise_dtypes=True)
        e.iota(t.iota_f, [[1, REL * WIN]], base=0, channel_multiplier=0, **big).then_inc(s_io, 1)
        e.iota(t.iota_pf, [[0, 1]], base=0, channel_multiplier=1, **big).then_inc(s_io, 1)
        e.iota(t.iota_h, [[1, BLOCKS * WIN]], base=0, channel_multiplier=0, **big).then_inc(s_io, 1)
        e.memset(p.ident[:, :], 0.0).then_inc(s_io, 1)
        e.wait_ge(s_io, 4)
        e.affine_select(out=p.ident[:, :], in_=p.ident[:, :], compare_op=ALU.not_equal, fill=1.0,
                        base=0, pattern=[[-1, P]], channel_multiplier=1).then_inc(s_io, 1)

    @block.vector
    def _(e):
        v = Tally(p.sem("prep"))
        e.wait_ge(s_ld, 13 * 16)
        v.inc(e.tensor_copy(t.typf, t.typ))
        v.inc(e.tensor_copy(t.dstf, t.dst))
        v.inc(e.tensor_copy(t.gbf, t.gbase))
        v.inc(e.tensor_scalar(t.shi, t.src, 7, None, ALU.arith_shift_right))
        v.inc(e.tensor_scalar(t.slo, t.src, P - 1, None, ALU.bitwise_and))
        v.inc(e.memset(t.bad, 0.0))
        v.inc(e.memset(t.ones, 1.0))
        v.link(e, e.memset(p.flag[:, :], 0))
        v.inc(e.tensor_copy(t.edge2[:, 0, :], t.slo))
        v.inc(e.tensor_copy(t.shif, t.shi))
        v.link(e, e.tensor_tensor(t.dloc.rearrange("p (g k) -> p g k", k=GT),
                                  t.dstf.rearrange("p (g k) -> p g k", k=GT),
                                  bcast(t.gbf, P, GT, GPAD), ALU.subtract))
        v.inc(e.scalar_tensor_tensor(t.edge2[:, 1, :], t.shif, float(WIN), t.dloc, ALU.mult, ALU.add))
        full = t.dloc[:, 0:TILES - 1]
        v.inc(e.tensor_reduce(t.red[:, 0:1], full, AX.X, ALU.max))
        v.inc(e.tensor_reduce(t.red[:, 1:2], full, AX.X, ALU.min))
        groups = TILES // GT + 1
        v.inc(e.tensor_tensor(t.gdiff[:, 0:groups - 3], t.gbf[:, 3:groups], t.gbf[:, 0:groups - 3],
                              ALU.subtract))
        v.inc(e.tensor_reduce(t.red[:, 3:4], t.gains[:, 0:3], AX.XY, ALU.max, apply_absolute_value=True))
        v.link(e, e.tensor_reduce(t.red[:, 4:5], t.gains[:, 3:6], AX.XY, ALU.max, apply_absolute_value=True))
        v.inc(e.tensor_reduce(t.red[:, 2:3], t.gdiff[:, 0:groups - 3], AX.X, ALU.min))
        v.link(e, e.scalar_tensor_tensor(t.red[:, 6:7], t.red[:, 3:4], float(HID) ** 0.5, t.red[:, 4:5],
                                         ALU.mult, ALU.add))
        v.inc(e.tensor_scalar(t.bad[:, 0:1], t.red[:, 0:1], float(WIN - 1), None, ALU.is_gt))
        v.inc(e.tensor_scalar(t.bad[:, 1:2], t.red[:, 1:2], 0.0, None, ALU.is_lt))
        v.inc(e.tensor_scalar(t.bad[:, 2:3], t.red[:, 2:3], 0.0, None, ALU.is_le))
        v.inc(e.tensor_scalar(t.bad[:, 3:4], t.red[:, 6:7], F16_TOP / SCALE, None, ALU.is_gt))
        last = t.dloc[0:LAST, TILES - 1:TILES]
        v.inc(e.tensor_scalar(t.bad[0:LAST, 5:6], last, float(WIN - 1), None, ALU.is_gt))
        v.inc(e.tensor_scalar(t.bad[0:LAST, 6:7], last, 0.0, None, ALU.is_lt))
        e.wait_ge(v.sem, v.n)
        e.sem_inc(s_sq)
        e.wait_ge(s_ps, 1)
        v.link(e, e.tensor_reduce(t.red[0:1, 8:9], p.psum[0:1, 0, 0:8], AX.X, ALU.max))
        v.link(e, e.tensor_scalar(p.flag[:, :], t.red[0:1, 8:9], 0.0, None, ALU.is_gt))
        e.wait_ge(s_sq, 2)
        v.link(e, e.tensor_scalar(t.sig[:, 0:3], t.sig[:, 0:3], 1.0, None, ALU.add))
        v.link(e, e.reciprocal(p.small[:, 0:3], t.sig[:, 0:3]))

    @block.scalar
    def _(e):
        e.wait_ge(s_ld, 13 * 16)
        e.wait_ge(s_sq, 1)
        e.activation(t.sig[:, 0:3], t.sig[:, 0:3], ACT.Exp, scale=-1.0).then_inc(s_sq, 1)

    @block.tensor
    def _(e):
        e.wait_ge(s_sq, 1)
        e.matmul(p.psum[0:1, 0, 0:8], t.ones[:, 0:1], t.bad[:, :], start=True, stop=True).then_inc(s_ps, 1)
    return block


GW, NW = 400, NPAD // 400


def one_hot_of_dst(t, k):
    return "vector", lambda e, i: e.tensor_scalar(t.gen_oh, t.gen_iota, t.gen_dst[:, k:k + 1], None, ALU.is_equal)


def place_of_dst(t, column):
    return "vector", lambda e, i: e.tensor_tensor(
        t.gen_dst, column(i).to_broadcast([P, NW]), t.gen_starts, ALU.subtract)


def general_constants(p, t, block, s_go):
    @block.gpsimd
    def _(e):
        big = dict(allow_small_or_imprecise_dtypes=True)
        e.iota(t.gen_iota, [[1, GW]], base=0, channel_multiplier=0, **big).then_inc(s_go, 1)
        e.iota(t.gen_starts, [[GW, NW]], base=0, channel_multiplier=0, **big).then_inc(s_go, 1)


def count_relations_general(p, t):
    s_go = p.sem("constants")
    block = Bodies()
    general_constants(p, t, block, s_go)
    steps = [("vector", lambda e, i: e.tensor_tensor(
                  t.gen_rel, t.iota_f[:, 0:32], t.typf[:, bass.ds(i, 1)].to_broadcast([P, 32]), ALU.is_equal)),
             place_of_dst(t, lambda i: t.dstf[:, bass.ds(i, 1)])]
    for k in range(NW):
        at = t.cnt[:, k * GW:(k + 1) * GW]
        steps += [one_hot_of_dst(t, k),
                  ("tensor", lambda e, i: e.matmul(p.psum[0:32, 0, 0:GW], t.gen_rel, t.gen_oh, start=True, stop=True)),
                  ("vector", lambda e, i, at=at: e.tensor_tensor(at, at, p.psum[0:32, 0, 0:GW], ALU.add))]
    loop = Serial(p, steps, TPAD)
    s_z = p.sem("zeroed")

    @block.vector
    def _(e):
        e.wait_ge(s_go, 2)
        e.memset(t.cnt, 0.0).then_inc(s_z, 1)
        e.wait_ge(s_z, 1)
        loop.body(e, "vector")

    @block.tensor
    def _(e):
        loop.body(e, "tensor")
    return block


def edge_weights_general(p, t):
    nc, d = p.nc, p.d
    s_dg, s_sq, s_st = p.sem("degrees"), p.sem("root"), p.sem("stored")
    block = Bodies()
    steps = [("vector", lambda e, i: e.tensor_tensor(
                  t.gen_rel, t.iota_f[:, 0:32], t.typf[:, bass.ds(i, 1)].to_broadcast([P, 32]), ALU.is_equal)),
             ("tensor", lambda e, i: e.transpose(p.psum[0:32, 1, 0:P], t.gen_rel, p.ident[:, :])),
             ("vector", lambda e, i: e.tensor_copy(t.gen_relt, p.psum[0:32, 1, 0:P])),
             place_of_dst(t, lambda i: t.dstf[:, bass.ds(i, 1)])]
    for k in range(NW):
        steps += [one_hot_of_dst(t, k),
                  ("tensor", lambda e, i, k=k: e.matmul(p.psum[:, 0, 0:GW], t.gen_relt, t.cnt[:, k * GW:(k + 1) * GW],
                                                        start=True, stop=True)),
                  ("vector", lambda e, i: e.tensor_tensor(t.gen_oh, t.gen_oh, p.psum[:, 0, 0:GW], ALU.mult)),
                  ("vector", lambda e, i, k=k: e.tensor_reduce(t.gen_part[:, k:k + 1], t.gen_oh, AX.X, ALU.add))]
    steps += [("vector", lambda e, i: e.tensor_reduce(t.gen_sum, t.gen_part, AX.X, ALU.add)),
              ("vector", lambda e, i: e.tensor_copy(t.wgt[:, bass.ds(i, 1)], t.gen_sum))]
    loop = Serial(p, steps, TPAD)

    @block.sync
    def _(e):
        store_weights(e, p, t, s_dg, s_st)

    @block.vector
    def _(e):
        v = Tally(p.sem("tail"))
        loop.body(e, "vector")
        finish_weights(e, v, p, t, s_dg, s_sq)

    @block.scalar
    def _(e):
        root_of_degree(e, t, s_dg, s_sq)

    @block.tensor
    def _(e):
        sum_degrees(e, p, t, s_dg)
        loop.body(e, "tensor")
    return block


def store_weights(e, p, t, s_dg, s_st):
    e.wait_ge(s_dg, 2)
    e.dma_start(p.d["w_pt"][:, :], t.wgt).then_inc(s_st, 16)
    e.wait_ge(s_st, 16)


def finish_weights(e, v, p, t, s_dg, s_sq):
    v.link(e, e.tensor_scalar(t.wgt, t.wgt, 1.0, None, ALU.max))
    v.link(e, e.reciprocal(t.wgt, t.wgt))
    e.wait_ge(s_dg, 1)
    v.link(e, e.tensor_scalar(t.deg, p.psum[:, 7, 0:BLOCKS], 1.0, None, ALU.add))
    e.sem_inc(s_dg)
    e.wait_ge(s_sq, 1)
    inverse_root(v, e, t.degr, t.deg, t.degt)
    for k, f in ((1, SCALE), (3, 1 / SCALE)):
        v.inc(e.tensor_scalar(p.cols[:, k, :], t.degr, f, None, ALU.mult))
    e.wait_ge(v.sem, v.n)


def root_of_degree(e, t, s_dg, s_sq):
    e.wait_ge(s_dg, 2)
    e.activation(t.degr, t.deg, ACT.Sqrt).then_inc(s_sq, 1)


def sum_degrees(e, p, t, s_dg):
    for b in range(BLOCKS):
        m = e.matmul(p.psum[:, 7, b:b + 1], t.cnt[:, b * P:(b + 1) * P], t.ones[0:32, 0:1], start=True, stop=True)
    m.then_inc(s_dg, 1)


def count_relations(p, t):
    nc = p.nc
    PER = 16
    G = PER // GT
    s_oh, s_mm = p.sem("onehots"), p.sem("counted")
    block = Bodies()

    @block.vector
    def _(e):
        v = Tally(s_oh)
        v.link(e, e.memset(t.cnt, 0.0))
        first = v.n
        regs = [e.alloc_register(f"cnt_base{k}") for k in range(G)]
        with e.Fori(0, TPAD // PER) as i:
            v.enter(i, 2 + G)
            e.wait_ge(s_mm, i * G + 1)
            v.inc(e.tensor_tensor(t.oh_r.rearrange("p (t r) -> p t r", r=32),
                                  t.iota_f[:, 0:32].rearrange("p (o r) -> p o r", o=1).to_broadcast([P, PER, 32]),
                                  bcast(t.typf[:, bass.ds(i * PER, PER)], P, 32, PER), ALU.is_equal))
            v.inc(e.tensor_tensor(t.oh_c.rearrange("p (t w) -> p t w", w=WIN),
                                  t.iota_f[:, 0:WIN].rearrange("p (o r) -> p o r", o=1).to_broadcast([P, PER, WIN]),
                                  bcast(t.dloc[:, bass.ds(i * PER, PER)], P, WIN, PER), ALU.is_equal))
            e.load(regs, t.gbase[0:1, bass.ds(i * G, G)])
            for g in range(G):
                base = e.snap(regs[g], min_val=0, max_val=NODES - 1)
                at = t.cnt[:, bass.ds(base, WIN)]
                e.wait_ge(s_mm, i * G + g + 2)
                v.link(e, e.tensor_tensor(at, at, p.psum[0:32, g, 0:WIN], ALU.add))
            v.leave(TPAD // PER)
        v.link(e, e.tensor_copy(t.cnt16, t.cnt))

    @block.tensor
    def _(e):
        e.sem_inc(s_mm)
        with e.Fori(0, TPAD // PER) as i:
            e.wait_ge(s_oh, i * (2 + G) + 3)
            for g in range(G):
                for k in range(g * GT, g * GT + GT):
                    m = e.matmul(p.psum[0:32, g, 0:WIN], t.oh_r[:, 32 * k:32 * k + 32],
                                 t.oh_c[:, WIN * k:WIN * k + WIN], start=(k % GT == 0), stop=(k % GT == GT - 1))
                m.then_inc(s_mm, 1)
    return block


def edge_weights(p, t):
    nc, d = p.nc, p.d
    PER, HALVES = 24, 2
    ROUNDS = TPAD // (PER * HALVES)
    G = PER // GT
    s_ld = [p.sem("types0"), p.sem("types1")]
    s_oh, s_mm, s_dg, s_sq, s_st = p.sem("onehots"), p.sem("fetched"), p.sem("degrees"), p.sem("root"), p.sem("stored")
    block = Bodies()

    @block.sync
    def _(e):
        def fetch(n, h):
            e.dma_start(t.rels[:, h * PER * P:(h + 1) * PER * P],
                        d["typ_rows"][bass.ds(n, 1), :].to_broadcast([32, PER * P])).then_inc(s_ld[h], 16)
        for h in range(HALVES):
            fetch(h, h)
        with e.Fori(0, ROUNDS - 1) as i:
            for h in range(HALVES):
                e.wait_ge(s_oh, i * HALVES * 4 + h * 4 + 1)
                fetch(i * HALVES + HALVES + h, h)
        store_weights(e, p, t, s_dg, s_st)

    @block.vector
    def _(e):
        v = Tally(s_oh)
        with e.Fori(0, ROUNDS) as i:
            v.enter(i, 4 * HALVES)
            for h in range(HALVES):
                n = i * HALVES + h
                e.wait_ge(s_mm, n + 1)
                e.wait_ge(s_ld[h], i * 16 + 16)
                v.inc(e.tensor_scalar(t.oh_t, t.rels[:, h * PER * P:(h + 1) * PER * P],
                                      t.iota_pf[0:32, :], None, ALU.is_equal))
                v.link(e, e.tensor_tensor(t.oh_w.rearrange("p (t w) -> p t w", w=WIN),
                                  t.iota_f[:, 0:WIN].rearrange("p (o r) -> p o r", o=1).to_broadcast([P, PER, WIN]),
                                  bcast(t.dloc[:, bass.ds(n * PER, PER)], P, WIN, PER), ALU.is_equal))
                e.wait_ge(s_mm, n + 2)
                for q in range(2):
                    half = t.oh_w[:, q * 12 * WIN:(q + 1) * 12 * WIN]
                    op = e.tensor_tensor(half, half, p.psum[:, q, 0:12 * WIN], ALU.mult)
                v.link(e, op)
                v.link(e, e.tensor_reduce(t.wgt[:, bass.ds(n * PER, PER)],
                                          t.oh_w.rearrange("p (t w) -> p t w", w=WIN), AX.X, ALU.add))
            v.leave(ROUNDS)
        finish_weights(e, v, p, t, s_dg, s_sq)

    @block.scalar
    def _(e):
        root_of_degree(e, t, s_dg, s_sq)

    @block.tensor
    def _(e):
        sum_degrees(e, p, t, s_dg)
        e.sem_inc(s_mm)
        regs = [e.alloc_register(f"w_base{k}") for k in range(G)]
        with e.Fori(0, ROUNDS) as i:
            for h in range(HALVES):
                n = i * HALVES + h
                e.load(regs, t.gbase[0:1, bass.ds(n * G, G)])
                e.wait_ge(s_oh, n * 4 + 2)
                for g in range(G):
                    base = e.snap(regs[g], min_val=0, max_val=NODES - 1)
                    for k in range(g * GT, g * GT + GT):
                        m = e.matmul(p.psum[:, k // 12, (k % 12) * WIN:(k % 12 + 1) * WIN],
                                     t.oh_t[:, k * P:(k + 1) * P], t.cnt16[:, bass.ds(base, WIN)],
                                     start=True, stop=True)
                m.then_inc(s_mm, 1)
    return block


def inverse_root(v, e, out, value, tmp):
    v.link(e, e.reciprocal(out, out))
    v.link(e, e.tensor_tensor(tmp, out, out, ALU.mult))
    v.link(e, e.tensor_tensor(tmp, tmp, value, ALU.mult))
    v.link(e, e.tensor_scalar(tmp, tmp, -0.5, 1.5, ALU.mult, ALU.add))
    v.link(e, e.tensor_tensor(out, out, tmp, ALU.mult))


def moments(v, e, x, stats, mv, n, passed):
    for k in range(n):
        v.inc(e.bn_stats(stats[:, k, :], x[:, k, :]))
    held(e, v.sem, v.now(), passed)
    for k in range(n):
        v.inc(e.bn_aggr(mv[:, k, :], stats[:, k, :]))
    e.wait_ge(v.sem, v.now())


def first_norm(p, t):
    nc, d = p.nc, p.d
    s_ld, s_v, s_sq, s_st = p.sem("x"), p.sem("norm"), p.sem("roots"), p.sem("stored")
    whole = (BLOCKS - 1) * P
    block = Bodies()

    @block.sync
    def _(e):
        e.dma_start(t.x[:, 0:BLOCKS - 1, :], d["x"][0:whole, :].rearrange("(b p) f -> p b f", p=P)).then_inc(s_ld, 16)
        e.wait_ge(s_v, 1)
        e.dma_start(t.x[0:NODES - whole, BLOCKS - 1, :], d["x"][whole:NODES, :]).then_inc(s_ld, 16)
        e.wait_ge(s_sq, 3)
        e.dma_start(d["x_pad"].rearrange("(b p) f -> p b f", p=P), t.x).then_inc(s_st, 16)
        e.dma_start(d["h16_0"].rearrange("(b p) h f -> p b (h f)", p=P),
                    t.h0[:, :, :, :].rearrange("p b h f -> p b (h f)")).then_inc(s_st, 16)
        e.wait_ge(s_st, 32)

    @block.vector
    def _(e):
        v = Tally(s_v)
        v.inc(e.memset(t.x[:, BLOCKS - 1, :], 0.0))
        e.wait_ge(s_ld, 32)
        moments(v, e, t.x, t.stats, t.mv, BLOCKS, p.sem("passed"))
        v.link(e, e.tensor_scalar(t.var, t.mv[:, :, 1], EPS, None, ALU.add))
        e.sem_inc(s_sq)
        e.wait_ge(s_sq, 2)
        inverse_root(v, e, t.rstd, t.var, t.tmp)
        for b in range(BLOCKS):
            v.inc(e.tensor_scalar(t.y[:, b, :], t.x[:, b, :], t.mv[:, b, 0:1], t.rstd[:, b:b + 1],
                                  ALU.subtract, ALU.mult))
        e.wait_ge(s_v, v.n)
        for b in range(BLOCKS):
            v.inc(e.tensor_scalar(t.y[:, b, :], t.y[:, b, :], 0.0, p.cols[:, 1, b:b + 1], ALU.max, ALU.mult))
        e.wait_ge(s_v, v.n)
        v.link(e, e.tensor_copy(t.h0[:, :, 0, :], t.y))
        v.link(e, e.tensor_tensor(t.h0[:, :, 1, :], t.y, t.h0[:, :, 0, :], ALU.subtract))
        e.sem_inc(s_sq)

    @block.scalar
    def _(e):
        e.wait_ge(s_sq, 1)
        e.activation(t.rstd, t.var, ACT.Sqrt).then_inc(s_sq, 1)
    return block


def norm_memory(p):
    t = Bag()
    c = p.carve(26000)
    t.x = c(BLOCKS * RF).rearrange("p (b f) -> p b f", b=BLOCKS)
    t.y = c(BLOCKS * RF).rearrange("p (b f) -> p b f", b=BLOCKS)
    t.h0 = c(BLOCKS * RF, F16).rearrange("p (b h f) -> p b h f", b=BLOCKS, h=2)
    t.stats = c(BLOCKS * 6).rearrange("p (b s) -> p b s", b=BLOCKS)
    t.mv = c(BLOCKS * 2).rearrange("p (b s) -> p b s", b=BLOCKS)
    t.var, t.rstd, t.tmp = c(BLOCKS), c(BLOCKS), c(BLOCKS)
    return t


def build_adjacency(p, t):
    nc = p.nc
    PER = 8
    G = PER // GT
    ROUNDS = EDGE_TILES // PER
    adj = p.arena[:, :].rearrange("p (b n) -> p b n", b=BLOCKS)
    N = BLOCKS * WIN
    H1 = 512 // WIN * WIN
    s_oh, s_sl, s_mm, s_ad, s_z = p.sem("keys"), p.sem("sources"), p.sem("outer"), p.sem("added"), p.sem("zeroed")
    block = Bodies()

    @block.gpsimd
    def _(e):
        e.memset(adj[:, BLOCKS // 2:, :], 0.0).then_inc(s_z, 1)

    @block.vector
    def _(e):
        v = Tally(s_ad)
        v.inc(e.memset(adj[:, 0:BLOCKS // 2, :], 0.0))
        v.inc(e.tensor_copy(t.iota_s, t.iota_h[:, 0:P]))
        e.wait_ge(s_ad, 2)
        e.wait_ge(s_z, 1)
        for b in range(BLOCKS):
            v.inc(e.tensor_copy(adj[:, b, b * P:(b + 1) * P], p.ident[:, :]))
        e.wait_ge(s_ad, v.n)
        n0 = v.n
        regs = [e.alloc_register(f"adj_base{k}") for k in range(G)]
        e.sem_inc(s_oh)

        def adds(i, first):
            e.load(regs, t.gbase[0:1, bass.ds(i * G, G)])
            for g in range(G):
                base = e.snap(regs[g], min_val=0, max_val=NODES - 1)
                e.wait_ge(s_mm, i * G + g + 2)
                for lo, hi, bank in ((0, H1 // WIN, 0), (H1 // WIN, BLOCKS, 1)):
                    at = adj[:, lo:hi, bass.ds(base, WIN)]
                    got = p.psum[:, 2 * g + bank, 0:(hi - lo) * WIN].rearrange("p (b w) -> p b w", w=WIN)
                    op = e.tensor_tensor(at, got, at, ALU.add)
                v.link(e, op)

        with e.Fori(0, ROUNDS) as i:
            v.enter(i, PER + 1 + G)
            e.wait_ge(s_mm, i * G + 1)
            v.link(e, e.tensor_copy(t.stage.rearrange("p (a t) -> p a t", a=2), t.edge2[:, :, bass.ds(i * PER, PER)]))
            for k in range(PER):
                v.inc(e.tensor_scalar(t.oh_s[:, k, :], t.iota_s, t.stage[:, k:k + 1], None, ALU.is_equal))
                op = e.tensor_scalar(t.oh_k[:, k, :], t.iota_h, t.stage[:, PER + k:PER + k + 1], None, ALU.is_equal)
                op.then_inc(s_oh, 1)
            adds(i, False)
            v.leave(ROUNDS)

    @block.tensor
    def _(e):
        e.sem_inc(s_mm)
        with e.Fori(0, ROUNDS) as i:
            for g in range(G):
                e.wait_ge(s_oh, i * PER + (g + 1) * GT + 1)
                for k in range(g * GT, g * GT + GT):
                    a, z = (k % GT == 0), (k % GT == GT - 1)
                    e.matmul(p.psum[:, 2 * g, 0:H1], t.oh_s[:, k, :], t.oh_k[:, k, 0:H1], start=a, stop=z)
                    m = e.matmul(p.psum[:, 2 * g + 1, 0:N - H1], t.oh_s[:, k, :], t.oh_k[:, k, H1:N],
                                 start=a, stop=z)
                m.then_inc(s_mm, 1)
    return block


def adjacency_memory(p, t):
    h = p.h16[:, :, :, :].rearrange("p a b c -> p (a b c)").bitcast(F32)
    t.edge2 = h[:, 0:2 * TPAD].rearrange("p (a t) -> p a t", a=2)
    t.iota_s = h[:, 1932:1996].bitcast(F16)
    t.stage = h[:, 1996:2012]
    t.oh_s = h[:, 2012:2012 + 512].bitcast(F16).rearrange("p (k s) -> p k s", k=8)
    t.oh_k = h[:, 2524:2524 + 2400].bitcast(F16).rearrange("p (k s) -> p k s", k=8)
    return t


GB = 5
GROUPS = BLOCKS // GB
GN = GB * P


def general_gcn_memory(p):
    t = Bag()
    edges = edge_columns(p)
    t.src, t.dstf = edges.src, edges.dstf
    c = p.carve(26000)
    t.sums = c(2 * NPAD).rearrange("p (k n) -> p k n", k=2)
    t.gen_idx, t.gen_to, t.gen_nodes = c(TPAD + BLOCKS, I32), c(TPAD + BLOCKS), c(BLOCKS, I32)
    t.gen_oh, t.gen_iota, t.gen_dst, t.gen_starts = c(GW), c(GW), c(NW), c(NW)
    t.pick, t.halves, t.row = c(1, I32), c(HID, F16), c(HID)
    return t


def general_aggregate(p, t, l, kh):
    fin = kh * P
    steps = [("vector", lambda e, i: e.tensor_copy(t.pick, t.gen_idx[:, bass.ds(i, 1)])),
             ("gpsimd", lambda e, i: e.indirect_dma_start(
                 out=t.halves[:, 0:2 * fin], out_offset=None, in_=p.d[f"h16_{l}"].rearrange("n h f -> n (h f)"),
                 in_offset=bass.IndirectOffsetOnAxis(ap=t.pick, axis=0))),
             ("vector", lambda e, i: e.tensor_tensor(t.row[:, 0:fin], t.halves[:, 0:fin], t.halves[:, fin:2 * fin],
                                                     ALU.add)),
             place_of_dst(t, lambda i: t.gen_to[:, bass.ds(i, 1)])]
    for k in range(NW):
        steps.append(one_hot_of_dst(t, k))
        for f in range(kh):
            at = t.sums[:, f, k * GW:(k + 1) * GW]
            steps += [("tensor", lambda e, i, f=f: e.matmul(p.psum[:, 0, 0:GW], t.row[:, f * P:(f + 1) * P], t.gen_oh,
                                                            start=True, stop=True)),
                      ("vector", lambda e, i, at=at: e.tensor_tensor(at, at, p.psum[:, 0, 0:GW], ALU.add))]
    return Serial(p, steps, TPAD + BLOCKS)


def gcn_layer(p, l, fast):
    nc, d = p.nc, p.d
    last = l == 3
    fin, fout = (RF if l == 0 else HID), (RF if last else HID)
    KH = fin // P
    h = p.h16[:, :, :, :].rearrange("p b h f -> p (b h f)")[:, 0:BLOCKS * 2 * fin].rearrange(
        "p (b h f) -> p b h f", b=BLOCKS, h=2)
    adj = p.arena[:, :].rearrange("p (b n) -> p b n", b=BLOCKS)
    work = p.work[:, :]
    zt = work[:, 0:2 * GN].rearrange("p (k n) -> p k n", k=2)
    u = work[:, 2 * GN:2 * GN + GB * fout].rearrange("p (b f) -> p b f", b=GB)
    ex = work[:, 4 * GN:4 * GN + GB * fout].rearrange("p (b f) -> p b f", b=GB)
    ho = work[:, 6 * GN:8 * GN].bitcast(F16).rearrange("p (b h f) -> p b h f", b=GB, h=2)
    xg = work[:, 6 * GN:7 * GN].rearrange("p (b f) -> p b f", b=GB)
    brow, gain, shift = (p.rows[:, k, 0:fout] for k in range(3))
    over = [r.rearrange("p (o f) -> p o f", o=1).to_broadcast([P, GB, fout]) for r in (gain, shift)]
    ln = p.lnbuf
    stats = ln[:, 0:6 * GB].rearrange("p (b s) -> p b s", b=GB)
    mv = ln[:, 30:40].rearrange("p (b s) -> p b s", b=GB)
    var, rstd, tmp, cs, ds = ln[:, 40:45], ln[:, 45:50], ln[:, 50:55], ln[:, 55:60], ln[:, 60:65]
    csig = p.csig[:, :]
    bank = p.psum[:, :, :].rearrange("p a b -> p (a b)")
    s_h, s_w, s_mm, s_v, s_a, s_vq, s_st, s_x = (p.sem(n) for n in (
        "inputs", "weights", "products", "node_ops", "scalar_ops", "asked", "stored", "x"))
    s_h2 = p.sem("second_part")
    passed = p.sem("passed")
    NM, NA = KH + 1, KH + (1 if last else 2)

    loop = t = None
    if not fast:
        t = general_gcn_memory(p)
        loop, s_go = general_aggregate(p, t, l, KH), p.sem("constants")
    block = Bodies()

    @block.sync
    def _(e):
        e.dma_start(h[:, 0:13].rearrange("p b h f -> p b (h f)"),
                    d[f"h16_{l}"][0:13 * P].rearrange("(b p) h f -> p b (h f)", p=P)).then_inc(s_h, 16)
        e.dma_start(p.wts[:, 0:KH, 0:fout], d[f"W{l}"].rearrange("(k p) o -> p k o", p=P)).then_inc(s_w, 16)
        e.dma_start(brow, d[f"b{l}"].partition_broadcast(P)).then_inc(s_w, 16)
        if not last:
            e.dma_start(gain, d[f"g{l}"].partition_broadcast(P)).then_inc(s_w, 16)
            e.dma_start(shift, d[f"beta{l}"].partition_broadcast(P)).then_inc(s_w, 16)
        with e.Fori(0, GROUPS) as i:
            rows = bass.ds(i * GN, GN)
            if last:
                e.wait_ge(s_st, i * 32 + 16)
                e.dma_start(xg, d["x_pad"][rows, :].rearrange("(b p) f -> p b f", p=P)).then_inc(s_x, 16)
                e.wait_ge(s_vq, i * 4 + 3)
                e.dma_start(d["x1"][rows, :].rearrange("(b p) f -> p b f", p=P), u).then_inc(s_st, 16)
                e.wait_ge(s_vq, i * 4 + 5)
                e.dma_start(d["rows_0"][rows, :].rearrange("(b p) f -> p b f", p=P), ex).then_inc(s_st, 16)
            else:
                e.wait_ge(s_vq, i * 4 + 5)
                e.dma_start(d[f"h16_{l + 1}"][rows].rearrange("(b p) h f -> p b (h f)", p=P),
                            ho.rearrange("p b h f -> p b (h f)")).then_inc(s_st, 16)
        e.wait_ge(s_st, 16 + GROUPS * (32 if last else 16))

    @block.gpsimd
    def _(e):
        e.dma_start(h[:, 13:].rearrange("p b h f -> p b (h f)"),
                    d[f"h16_{l}"][13 * P:].rearrange("(b p) h f -> p b (h f)", p=P)).then_inc(s_h2, 16)
        e.sem_inc(s_st, 16)
        e.wait_ge(s_h2, 16)
        if not fast:
            big = dict(allow_small_or_imprecise_dtypes=True)
            e.iota(t.gen_iota, [[1, GW]], base=0, channel_multiplier=0, **big).then_inc(s_go, 1)
            e.iota(t.gen_starts, [[GW, NW]], base=0, channel_multiplier=0, **big).then_inc(s_go, 1)
            e.iota(t.gen_nodes, [[P, BLOCKS]], base=0, channel_multiplier=1).then_inc(s_go, 1)
            loop.body(e, "gpsimd")

    @block.tensor
    def _(e):
        e.sem_inc(s_mm)
        e.wait_ge(s_h, 16)
        if not fast:
            loop.body(e, "tensor")
        nc.disable_value_cache = True
        with e.Fori(0, GROUPS) as i:
            for k in range(KH):
                if not fast:
                    e.wait_ge(s_vq, i * 4 + 1)
                    e.sem_inc(s_mm)
                    continue
                e.wait_ge(s_a, i * NA + k + 1)
                for b in range(BLOCKS):
                    if b == 13:
                        e.wait_ge(s_h2, 16)
                    for half in range(2):
                        a, z = (b == 0 and half == 0), (b == BLOCKS - 1 and half == 1)
                        wt = h[:, b, half, k * P:(k + 1) * P]
                        e.matmul(bank[:, 1024 * k:1024 * k + 512], wt, adj[:, b, bass.ds(i * GN, 512)],
                                 start=a, stop=z)
                        m = e.matmul(bank[:, 1024 * k + 512:1024 * k + GN], wt,
                                     adj[:, b, bass.ds(i * GN + 512, GN - 512)], start=a, stop=z)
                m.then_inc(s_mm, 1)
            e.wait_ge(s_w, 16 * (2 if last else 4))
            e.wait_ge(s_a, i * NA + NA + KH)
            e.wait_ge(s_vq, i * 4 + 1)
            for b in range(GB):
                for k in range(KH):
                    m = e.matmul(bank[:, 2048 + b * 256:2048 + b * 256 + fout], zt[:, k, b * P:(b + 1) * P],
                                 p.wts[:, k, 0:fout], start=(k == 0), stop=(k == KH - 1))
            m.then_inc(s_mm, 1)
        nc.disable_value_cache = False

    @block.scalar
    def _(e):
        if not fast:
            e.wait_ge(loop.done, loop.iterations * len(loop.steps) + 1)
        e.sem_inc(s_a, NA)
        with e.Fori(0, GROUPS) as i:
            held(e, s_mm, i * NM + 1, passed)
            for k in range(KH):
                held(e, s_mm, i * NM + k + 2, passed)
                got = bank[:, 1024 * k:1024 * k + GN] if fast else t.sums[:, k, bass.ds(i * GN, GN)]
                e.activation(zt[:, k, :], got, ACT.Copy).then_inc(s_a, 1)
            held(e, s_vq, i * 4 + 3, passed)
            e.activation(rstd, var, ACT.Sqrt).then_inc(s_a, 1)
            if not last:
                held(e, s_vq, i * 4 + 4, passed)
                e.activation(ex, ex, ACT.Exp).then_inc(s_a, 1)

    @block.vector
    def _(e):
        v = Tally(s_v)
        if not fast:
            e.wait_ge(s_go, 3)
            v.inc(e.memset(t.sums, 0.0))
            v.inc(e.tensor_copy(t.gen_idx[:, 0:TPAD], t.src))
            v.inc(e.tensor_copy(t.gen_idx[:, TPAD:], t.gen_nodes))
            v.inc(e.tensor_copy(t.gen_to[:, 0:TPAD], t.dstf))
            v.link(e, e.tensor_copy(t.gen_to[:, TPAD:], t.gen_nodes))
            loop.body(e, "vector")
        e.wait_ge(s_w, 16 * (2 if last else 4))
        if last:
            v.link(e, e.tensor_copy(csig, p.cols[:, 3, :]))
        else:
            v.inc(e.tensor_scalar(csig, p.cols[:, 3, :], p.small[:, l:l + 1], None, ALU.mult))
            v.link(e, e.tensor_scalar(brow, brow, p.small[:, l:l + 1], None, ALU.mult))
        e.sem_inc(s_vq)
        per = (2 + GB + 1 + 2 * GB + 1 + 5 + GB + 1) if last else (2 + GB + 2 * GB + 1 + 5 + GB + 4 + GB + 2)
        with e.Fori(0, GROUPS) as i:
            v.enter(i, per)
            if not last:
                e.wait_ge(s_st, i * 16 + 16)
            else:
                e.wait_ge(s_st, i * 32 + 16)
            v.inc(e.tensor_copy(cs, csig[:, bass.ds(i * GB, GB)]))
            v.link(e, e.tensor_copy(ds, p.cols[:, 1, bass.ds(i * GB, GB)]))
            e.wait_ge(s_mm, i * NM + NM + 1)
            for b in range(GB):
                v.inc(e.scalar_tensor_tensor(u[:, b, :], bank[:, 2048 + b * 256:2048 + b * 256 + fout],
                                             cs[:, b:b + 1], brow, ALU.mult, ALU.add))
            e.wait_ge(s_v, v.now())
            e.sem_inc(s_vq)
            if last:
                e.wait_ge(s_x, i * 16 + 16)
                v.link(e, e.tensor_tensor(u, u, xg, ALU.add))
            moments(v, e, u, stats, mv, GB, passed)
            v.link(e, e.tensor_scalar(var, mv[:, :, 1], EPS, None, ALU.add))
            e.sem_inc(s_vq)
            e.wait_ge(s_a, i * NA + NA + KH + 1)
            inverse_root(v, e, rstd, var, tmp)
            to = ex if last else u
            for b in range(GB):
                v.inc(e.tensor_scalar(to[:, b, :], u[:, b, :], mv[:, b, 0:1], rstd[:, b:b + 1],
                                      ALU.subtract, ALU.mult))
            e.wait_ge(s_v, v.now())
            if last:
                e.sem_inc(s_vq)
                v.link(e, e.tensor_scalar(ex, ex, 0.0, None, ALU.max))
                e.sem_inc(s_vq)
            else:
                v.link(e, e.tensor_tensor(u, u, over[0], ALU.mult))
                v.link(e, e.tensor_tensor(u, u, over[1], ALU.add))
                v.link(e, e.tensor_scalar(ex, u, 0.0, None, ALU.min))
                e.sem_inc(s_vq)
                e.wait_ge(s_a, i * NA + NA + KH + 2)
                v.link(e, e.scalar_tensor_tensor(u, u, 0.0, ex, ALU.max, ALU.add))
                for b in range(GB):
                    v.inc(e.tensor_scalar(ex[:, b, :], u[:, b, :], -1.0, ds[:, b:b + 1], ALU.add, ALU.mult))
                e.wait_ge(s_v, v.now())
                v.link(e, e.tensor_copy(ho[:, :, 0, :], ex))
                v.link(e, e.tensor_tensor(ho[:, :, 1, :], ex, ho[:, :, 0, :], ALU.subtract))
                e.sem_inc(s_vq)
            v.leave(GROUPS)
    return block


ROUND = 16


def relation_memory(p):
    t = Bag()
    c = p.carve(0)
    t.hrows = c(NPAD).rearrange("p (b f) -> p b f", b=BLOCKS)
    t.ht, t.acc = c(NPAD), c(NPAD)
    t.wr = c(REL * RF).rearrange("p (r o) -> p r o", r=REL)
    t.root, t.bias = c(RF), c(1)
    t.idx, t.rels, t.dsti = c(EDGE_TILES, I32), c(EDGE_TILES, I32), c(EDGE_TILES, I32)
    t.gbase = c(GPAD, I32)
    t.typf, t.dstf, t.gbf = c(EDGE_TILES), c(EDGE_TILES), c(GPAD)
    t.edge2 = c(2 * EDGE_TILES).rearrange("p (a t) -> p a t", a=2)
    t.iota = c(REL * WIN)
    t.stage = c(2 * ROUND)
    t.oh = c(ROUND * REL * WIN).rearrange("p (k n) -> p k n", k=ROUND)
    t.msg = c(ROUND * RF).rearrange("p (k n) -> p k n", k=ROUND)
    t.pick = c(ROUND, I32)
    t.agg = c(REL * ROUND // GT * WIN).rearrange("p (r g w) -> p r g w", r=REL, g=ROUND // GT)
    t.gen_oh, t.gen_iota, t.gen_dst, t.gen_starts = c(GW), c(GW), c(NW), c(NW)
    t.gen_rel, t.gen_types, t.gen_to, t.gen_y = c(REL), c(EDGE_TILES), c(EDGE_TILES), c(REL * RF)
    t.x1 = c(NPAD).rearrange("p (b f) -> p b f", b=BLOCKS)
    return t


def relation_setup(p, t):
    nc, d = p.nc, p.d
    s_ld, s_io, s_tr, s_ev, s_r = p.sem("loaded"), p.sem("iota"), p.sem("transposed"), p.sem("evacuated"), p.sem("rows")
    block = Bodies()

    @block.sync
    def _(e):
        e.dma_start(t.dsti, d["dst_pt"][:, 0:EDGE_TILES]).then_inc(s_ld, 16)
        e.dma_start(t.rels, d["typ_pt"][:, 0:EDGE_TILES]).then_inc(s_ld, 16)
        e.dma_start(t.gbase, d["gbase"].partition_broadcast(P)).then_inc(s_ld, 16)
        e.dma_start(t.idx, d["src_pt"][:, 0:EDGE_TILES]).then_inc(s_ld, 16)
        e.dma_start(t.edge2[:, 1, :], d["w_pt"][:, 0:EDGE_TILES]).then_inc(s_ld, 16)
        e.dma_start(t.hrows, d["rows_0"].rearrange("(b p) f -> p b f", p=P)).then_inc(s_r, 16)
        e.wait_ge(s_ld, 5 * 16)
        e.wait_ge(s_r, 16)

    @block.gpsimd
    def _(e):
        e.iota(t.iota, [[1, REL * WIN]], base=0, channel_multiplier=0,
               allow_small_or_imprecise_dtypes=True).then_inc(s_io, 1)

    @block.vector
    def _(e):
        v = Tally(p.sem("setup"))
        e.wait_ge(s_ld, 5 * 16)
        v.inc(e.tensor_copy(t.typf, t.rels))
        v.inc(e.tensor_copy(t.dstf, t.dsti))
        v.link(e, e.tensor_copy(t.gbf, t.gbase))
        v.link(e, e.tensor_tensor(t.dstf.rearrange("p (g k) -> p g k", k=GT),
                                  t.dstf.rearrange("p (g k) -> p g k", k=GT),
                                  bcast(t.gbf[:, 0:EDGE_TILES // GT], P, GT, EDGE_TILES // GT), ALU.subtract))
        v.inc(e.scalar_tensor_tensor(t.edge2[:, 0, :], t.typf, float(WIN), t.dstf, ALU.mult, ALU.add))
        e.wait_ge(s_io, 1)
        for g in range(7):
            n = min(4, BLOCKS - 4 * g)
            e.wait_ge(s_tr, g + 1)
            e.tensor_copy(t.ht[:, g * 512:g * 512 + n * P], p.psum[:, g, 0:n * P]).then_inc(s_ev, 1)

    @block.tensor
    def _(e):
        e.wait_ge(s_r, 16)
        for b in range(BLOCKS):
            m = e.transpose(p.psum[:, b // 4, (b % 4) * P:(b % 4 + 1) * P], t.hrows[:, b, :], p.ident[:, :])
            if b % 4 == 3 or b == BLOCKS - 1:
                m.then_inc(s_tr, 1)
    return block


def general_relations(p, t, l):
    y = p.psum[:, 2:6, :].rearrange("p a (c o) -> p (a c) o", o=RF)
    by_o = t.gen_y.rearrange("p (r o) -> p o r", r=REL)
    steps = [("vector", lambda e, i: e.tensor_copy(t.pick[:, 0:1], t.idx[:, bass.ds(i, 1)])),
             ("gpsimd", lambda e, i: e.indirect_dma_start(
                 out=t.msg[:, 0, :], out_offset=None, in_=p.d[f"rows_{l}"][:, :],
                 in_offset=bass.IndirectOffsetOnAxis(ap=t.pick[:, 0:1], axis=0))),
             ("tensor", lambda e, i: e.transpose(p.psum[:, 1, 0:P], t.msg[:, 0, :], p.ident[:, :])),
             ("vector", lambda e, i: e.tensor_copy(t.msg[:, 1, :], p.psum[:, 1, 0:P]))]
    for q in range(4):
        steps.append(("tensor", lambda e, i, q=q: e.matmul(
            p.psum[:, 2 + q, :], t.msg[:, 1, :], t.wr[:, 4 * q:4 * q + 4, :].rearrange("p r o -> p (r o)"),
            start=True, stop=True)))
    steps += [("vector", lambda e, i: e.tensor_tensor(
                  t.gen_rel, t.iota[:, 0:REL], t.gen_types[:, bass.ds(i, 1)].to_broadcast([P, REL]), ALU.is_equal)),
              ("vector", lambda e, i: e.tensor_tensor(
                  t.gen_rel, t.gen_rel, t.edge2[:, 1, bass.ds(i, 1)].to_broadcast([P, REL]), ALU.mult)),
              ("vector", lambda e, i: e.tensor_tensor(
                  t.gen_y.rearrange("p (r o) -> p r o", r=REL), y, bcast(t.gen_rel, P, RF, REL), ALU.mult)),
              ("vector", lambda e, i: e.tensor_reduce(t.msg[:, 2, :], by_o, AX.X, ALU.add)),
              place_of_dst(t, lambda i: t.gen_to[:, bass.ds(i, 1)])]
    for k in range(NW):
        at = t.acc[:, k * GW:(k + 1) * GW]
        steps += [one_hot_of_dst(t, k),
                  ("tensor", lambda e, i: e.matmul(p.psum[:, 0, 0:GW], t.msg[:, 2, :], t.gen_oh, start=True, stop=True)),
                  ("vector", lambda e, i, at=at: e.tensor_tensor(at, at, p.psum[:, 0, 0:GW], ALU.add))]
    return Serial(p, steps, EDGE_TILES)


def relation_layer(p, t, l, fast):
    nc, d = p.nc, p.d
    PER = ROUND
    G = PER // GT
    FULL = EDGE_TILES // PER
    REST = EDGE_TILES - FULL * PER
    last = l == 2
    s_ld, s_x1, s_rt, s_ac, s_pk, s_oh, s_ag, s_ev, s_ot, s_ad, s_fr = (p.sem(n) for n in (
        "weights", "x1", "root", "root_added", "picked", "onehots", "means", "evacuated", "outputs", "added", "freed"))
    s_got = [p.sem(f"rows{k}") for k in range(PER)]
    passed = p.sem("passed")
    loop = None
    if not fast:
        loop, s_go = general_relations(p, t, l), p.sem("constants")
    MEAN, OUT = 0, 4
    block = Bodies()

    @block.sync
    def _(e):
        e.dma_start(t.wr, d["W"][l].rearrange("r f o -> f r o")).then_inc(s_ld, 16)
        e.dma_start(t.root, d["root"][l]).then_inc(s_ld, 16)
        e.dma_start(t.bias, d["bias"][l].rearrange("(o b) -> o b", b=1)).then_inc(s_ld, 16)
        e.wait_ge(s_ld, 48)
        if last:
            e.dma_start(t.x1, d["x1"].rearrange("(b p) f -> p b f", p=P)).then_inc(s_x1, 16)
            e.wait_ge(s_x1, 16)

    @block.gpsimd
    def _(e):
        if not fast:
            big = dict(allow_small_or_imprecise_dtypes=True)
            e.iota(t.gen_iota, [[1, GW]], base=0, channel_multiplier=0, **big).then_inc(s_go, 1)
            e.iota(t.gen_starts, [[GW, NW]], base=0, channel_multiplier=0, **big).then_inc(s_go, 1)
            loop.body(e, "gpsimd")
            return

        def gather(i, k):
            held(e, s_pk, i * PER + k + 1, passed)
            e.indirect_dma_start(out=t.msg[:, k, :], out_offset=None, in_=d[f"rows_{l}"][:, :],
                                 in_offset=bass.IndirectOffsetOnAxis(ap=t.pick[:, k:k + 1], axis=0)
                                 ).then_inc(s_got[k], 16)
        with e.Fori(0, FULL) as i:
            for k in range(PER):
                gather(i, k)
        for k in range(REST):
            gather(FULL, k)

    def scalar(e):
        e.sem_inc(s_ev, G)

        def pick(i, k):
            e.activation(t.pick[:, k:k + 1], t.idx[:, bass.ds(i * PER + k, 1)], ACT.Copy).then_inc(s_pk, 1)

        def take(i, g):
            held(e, s_ag, i * PER + (g + 1) * GT + PER, passed)
            if g == 0:
                held(e, s_ot, i + 1, passed)
            e.activation(t.agg[:, :, g, :], p.psum[:, MEAN + g, 0:REL * WIN].rearrange("p (r w) -> p r w", r=REL),
                         ACT.Copy).then_inc(s_ev, 1)

        def turn(i, picks, takes):
            for k in range(takes * GT):
                if k < picks:
                    held(e, s_ag, i * PER + k + 1 + PER, passed)
                    pick(i + 1, k)
                if k % GT == GT - 1:
                    take(i, k // GT)

        for k in range(PER):
            pick(0, k)
        with e.Fori(0, FULL - 1) as i:
            turn(i, PER, G)
        turn(FULL - 1, REST, G)
        turn(FULL, 0, REST // GT)

    if fast:
        block.scalar(scalar)

    @block.vector
    def _(e):
        v = Tally(p.sem("out_adds"))
        regs = [e.alloc_register(f"out_base{l}_{int(fast)}_{k}") for k in range(G)]
        e.wait_ge(s_ld, 48)
        for g in range(7):
            n = min(512, NPAD - 512 * g)
            e.wait_ge(s_rt, g + 1)
            v.inc(e.tensor_scalar(t.acc[:, g * 512:g * 512 + n], p.psum[:, g, 0:n], t.bias[:, 0:1], None, ALU.add))
        e.wait_ge(v.sem, v.n)
        e.sem_inc(s_ac)

        def stage(i, n):
            e.wait_ge(s_oh, i * PER + 1)
            v.link(e, e.tensor_copy(t.stage.rearrange("p (a t) -> p a t", a=2)[:, :, 0:n],
                                    t.edge2[:, :, bass.ds(i * PER, n)]))

        def onehots(i, k0, k1):
            for k in range(k0, k1):
                e.wait_ge(s_ag, i * PER + k + 1)
                e.tensor_scalar(t.oh[:, k, :], t.iota, t.stage[:, k:k + 1], t.stage[:, PER + k:PER + k + 1],
                                ALU.is_equal, ALU.mult).then_inc(s_oh, 1)

        def adds(i, groups):
            e.load(regs[0:groups], t.gbase[0:1, bass.ds(i * G, groups)])
            e.wait_ge(s_ot, i + 2)
            for g in range(groups):
                base = e.snap(regs[g], min_val=0, max_val=NODES - 1)
                at = t.acc[:, bass.ds(base, WIN)]
                v.link(e, e.tensor_tensor(at, at, p.psum[:, OUT, g * WIN:(g + 1) * WIN], ALU.add))
            e.sem_inc(s_ad)

        if fast:
            e.sem_inc(s_oh)
            stage(0, PER)
            onehots(0, 0, PER)
            with e.Fori(0, FULL - 1) as i:
                v.enter(i, 1 + G)
                stage(i + 1, PER)
                onehots(i + 1, 0, PER // 2)
                adds(i, G)
                onehots(i + 1, PER // 2, PER)
                v.leave(FULL - 1)
            stage(FULL, REST)
            onehots(FULL, 0, REST)
            adds(FULL - 1, G)
            adds(FULL, REST // GT)
        else:
            e.wait_ge(s_go, 2)
            v.inc(e.tensor_copy(t.gen_types, t.typf))
            v.link(e, e.tensor_copy(t.gen_to, t.dsti))
            loop.body(e, "vector")
        if not last:
            v.link(e, e.tensor_scalar(t.ht, t.acc, 0.0, None, ALU.max))
        e.sem_inc(s_fr)
        for g in range(7):
            n = min(4, BLOCKS - 4 * g)
            e.wait_ge(s_fr, g + 2)
            part = p.psum[:, g, 0:n * P].rearrange("p (b f) -> p b f", b=n)
            if last:
                if g == 0:
                    e.wait_ge(s_x1, 16)
                v.inc(e.tensor_tensor(t.hrows[:, 4 * g:4 * g + n, :], part, t.x1[:, 4 * g:4 * g + n, :], ALU.add))
            else:
                v.inc(e.tensor_copy(t.hrows[:, 4 * g:4 * g + n, :], part))
        e.wait_ge(v.sem, v.n)
        e.sem_inc(s_ac)

    @block.tensor
    def _(e):
        e.wait_ge(s_ld, 48)
        for g in range(7):
            n = min(512, NPAD - 512 * g)
            e.matmul(p.psum[:, g, 0:n], t.root, t.ht[:, g * 512:g * 512 + n], start=True, stop=True).then_inc(s_rt, 1)
        e.wait_ge(s_ac, 1)
        if fast:
            e.sem_inc(s_ag, PER)
            e.sem_inc(s_ot)

            def work(i, groups):
                for g in range(groups):
                    e.wait_ge(s_ev, i * G + g + 1)
                    for k in range(g * GT, g * GT + GT):
                        e.wait_ge(s_got[k], i * 16 + 16)
                        e.wait_ge(s_oh, i * PER + k + 2)
                        e.matmul(p.psum[:, MEAN + g, 0:REL * WIN], t.msg[:, k, :], t.oh[:, k, :],
                                 start=(k % GT == 0), stop=(k % GT == GT - 1)).then_inc(s_ag, 1)
                e.wait_ge(s_ev, i * G + G + groups)
                e.wait_ge(s_ad, i + 1)
                for r in range(REL):
                    m = e.matmul(p.psum[:, OUT, 0:groups * WIN], t.wr[:, r, :],
                                 t.agg[:, r, 0:groups, :].rearrange("p g w -> p (g w)"),
                                 start=(r == 0), stop=(r == REL - 1))
                m.then_inc(s_ot, 1)
            e.sem_inc(s_ad)
            with e.Fori(0, FULL) as i:
                work(i, G)
            work(FULL, REST // GT)
        else:
            loop.body(e, "tensor")
        e.wait_ge(s_fr, 1)
        for b in range(BLOCKS):
            m = e.transpose(p.psum[:, b // 4, (b % 4) * P:(b % 4 + 1) * P],
                            (t.acc if last else t.ht)[:, b * P:(b + 1) * P], p.ident[:, :])
            if b % 4 == 3 or b == BLOCKS - 1:
                m.then_inc(s_fr, 1)
    return block


def store_rows(p, t, l):
    d, last = p.d, l == 2
    s_st = p.sem("stored")
    block = Bodies()

    @block.sync
    def _(e):
        if last:
            whole = (BLOCKS - 1) * P
            e.dma_start(d["out"][0:whole, :].rearrange("(b p) f -> p b f", p=P),
                        t.hrows[:, 0:BLOCKS - 1, :]).then_inc(s_st, 16)
            e.dma_start(d["out"][whole:NODES, :], t.hrows[0:NODES - whole, BLOCKS - 1, :]).then_inc(s_st, 16)
            e.wait_ge(s_st, 32)
        else:
            e.dma_start(d[f"rows_{l + 1}"].rearrange("(b p) f -> p b f", p=P), t.hrows).then_inc(s_st, 16)
            e.wait_ge(s_st, 16)
    return block


class Bag:
    pass


def edge_columns(p):
    t = Bag()
    h = p.h16[:, :, :, :].rearrange("p a b c -> p (a b c)").bitcast(F32)
    w = p.work[:, :]
    t.iota_h = h[:, 1632:1932].bitcast(F16)
    adjacency_memory(p, t)
    t.gbase = w[:, 0:GPAD].bitcast(I32)
    c = p.carve(0)
    t.typf, t.dstf, t.shif, t.dloc, t.wgt = (c(TPAD) for _ in range(5))
    t.src, t.dst, t.typ, t.shi, t.slo = (c(TPAD, I32) for _ in range(5))
    t.gbf, t.gdiff = c(GPAD), c(GPAD)
    t.iota_f, t.iota_pf = c(REL * WIN), c(1)
    t.gains = c(6 * HID).rearrange("p (k o) -> p k o", k=6)
    t.sig, t.red, t.bad, t.ones, t.deg = c(4), c(10), c(8), c(1), c(BLOCKS)
    t.degr, t.degt = c(BLOCKS), c(BLOCKS)
    t.cnt, t.cnt16 = c(NPAD, parts=32), c(NPAD // 2, F16, parts=32)
    t.oh_r, t.oh_c, t.oh_w = c(16 * 32 // 2, F16), c(16 * WIN // 2, F16), c(24 * WIN)
    t.rels, t.oh_t = c(48 * P, I32, parts=32), c(24 * P // 2, F16, parts=32)
    t.gen_oh, t.gen_iota, t.gen_dst, t.gen_starts = c(GW), c(GW), c(NW), c(NW)
    t.gen_rel, t.gen_relt, t.gen_part, t.gen_sum = c(32), c(P, parts=32), c(NW), c(1)
    assert p.at <= 26000, p.at
    return t


def scratch(nc, dram):
    def make(name, shape, dt):
        dram[name] = nc.dram_tensor(name, shape, dt).ap()
    make("w_pt", (P, TPAD), F32)
    make("x_pad", (NPAD, RF), F32)
    make("x1", (NPAD, RF), F32)
    for l in range(4):
        make(f"h16_{l}", (NPAD, 2, RF if l == 0 else HID), F16)
    for l in range(3):
        make(f"rows_{l}", (NPAD, RF), F32)


def build(nc, dram):
    with ExitStack() as ctx:
        p = Prog(nc, ctx, dram)
        scratch(nc, dram)
        t = edge_columns(p)
        run(p, prepare(p, t))
        run(p, count_relations(p, t), count_relations_general(p, t))
        run(p, edge_weights(p, t), edge_weights_general(p, t))
        run(p, first_norm(p, norm_memory(p)))
        run(p, build_adjacency(p, t), Bodies())
        for l in range(4):
            run(p, gcn_layer(p, l, True), gcn_layer(p, l, False))
        t = relation_memory(p)
        run(p, relation_setup(p, t))
        for l in range(3):
            run(p, relation_layer(p, t, l, True), relation_layer(p, t, l, False))
            run(p, store_rows(p, t, l))
_F32 = ["x", "g0", "g1", "g2", "beta0", "beta1", "beta2", "b0", "b1", "b2", "b3", "a0", "a1", "a2",
        "W0", "W1", "W2", "W3"]


def kernel(**inputs):
    import concourse.bacc as bacc
    from concourse.bass_utils import run_bass_kernel_spmd as run
    nc = bacc.Bacc("TRN2", target_bir_lowering=False, num_devices=1)
    given = {n: np.ascontiguousarray(inputs["x" if n == "x" else f"L0_gnn_{n}"]) for n in _F32}
    given["W"], given["root"], given["bias"] = (np.ascontiguousarray(inputs[f"L1_gnn_{n}"]) for n in ("W", "root", "bias"))

    def tiles(a, fill):
        flat = np.full(TPAD * P, fill, np.int32)
        flat[:EDGES] = a
        return flat

    src, dst, typ = tiles(inputs["src"], 0), tiles(inputs["dst"], -1), tiles(inputs["edge_type_16"], 0)
    for name, a in (("src", src), ("dst", dst), ("typ", typ)):
        given[name + "_pt"] = np.ascontiguousarray(a.reshape(TPAD, P).T)
    given["typ_rows"] = typ.reshape(-1, 24 * P)
    gbase = dst[::GT * P].copy()
    gbase[-(-TILES // GT):] = 0
    given["gbase"] = gbase
    dram = {}
    for n, a in given.items():
        dram[n] = nc.dram_tensor("in_" + n, a.shape, mybir.dt.from_np(a.dtype), kind="ExternalInput").ap()
    dram["out"] = nc.dram_tensor("out", (NODES, RF), F32, kind="ExternalOutput").ap()
    build(nc, dram)
    r = run(nc, [{"in_" + n: a for n, a in given.items()}], core_ids=[0])
    return r.results[0]["out"]
```

```python
import numpy as np
import concourse.bass as bass
from concourse import mybir
from contextlib import ExitStack

F32, F16, I32 = mybir.dt.float32, mybir.dt.float16, mybir.dt.int32
ALU = mybir.AluOpType
ACT = mybir.ActivationFunctionType
AX = mybir.AxisListType

P = 128
NODES, EDGES = 3125, 103125
BLOCKS = -(-NODES // P)
NPAD = BLOCKS * P
WIN = 20
TILES = -(-EDGES // P)
GT = 4
TPAD = 816
GPAD = TPAD // GT
CHUNK = 48
EDGE_TILES = 808
LAST = EDGES - (TILES - 1) * P
IN_F, HID, REL, RF = 128, 256, 16, 128
F16_TOP = 60000.0
SCALE = 16.0
SCALE3 = 4.0
EPS = 1e-5


class Tally:

    def __init__(self, sem):
        self.sem, self.n, self.loop = sem, 0, None

    def inc(self, ins):
        ins.then_inc(self.sem, 1)
        self.n += 1
        return ins

    def enter(self, i, per):
        self.loop = (i, per, self.n)

    def leave(self, iterations):
        i, per, n0 = self.loop
        assert self.n - n0 == per, (self.n - n0, per)
        self.n, self.loop = n0 + per * iterations, None

    def now(self):
        return self.n if self.loop is None else self.loop[0] * self.loop[1] + self.n

    def link(self, eng, ins):
        self.inc(ins)
        eng.wait_ge(self.sem, self.now())
        return ins


class Prog:

    def __init__(self, nc, ctx, dram):
        self.nc, self.ctx, self.d = nc, ctx, dram

        def sb(name, shape, dt):
            return ctx.enter_context(nc.sbuf_tensor(name, shape, dt))

        self.arena = sb("arena", [P, BLOCKS * NPAD], F16)
        self.h16 = sb("h16", [P, BLOCKS, 2, HID], F16)
        self.work = sb("work", [P, 4 * 5 * HID], F32)
        self.wts = sb("wts", [P, 2, HID], F32)
        self.rows = sb("rows", [P, 3, HID], F32)
        self.ident = sb("ident", [P, P], F32)
        self.cols = sb("cols", [P, 4, BLOCKS], F32)
        self.flag = sb("flag", [1, 1], I32)
        self.small = sb("small", [P, 4], F32)
        self.lnbuf = sb("lnbuf", [P, 68], F32)
        self.csig = sb("csig", [P, BLOCKS], F32)
        self.psum = ctx.enter_context(nc.psum_tensor("psum", [P, 8, 512], F32))
        self.n_sem, self.live = 0, []
        self.at = 0

    def sem(self, name):
        self.n_sem += 1
        handle = self.nc.alloc_semaphore(f"{name}_{self.n_sem}")
        self.live.append(handle)
        return handle

    def end_stage(self):
        self.nc.clear_and_free_semaphores(self.live)
        self.nc.all_engine_barrier()
        self.live = []

    def carve(self, start=None):
        if start is not None:
            self.at = start
        whole = self.arena[:, :].bitcast(F32)

        def piece(words, dt=F32, parts=P):
            a = whole[0:parts, self.at:self.at + words]
            self.at += words
            assert self.at <= BLOCKS * NPAD // 2, self.at
            return a if dt == F32 else a.bitcast(dt)
        return piece


class Bodies:

    def __init__(self):
        self.of = {}

    def sync(self, f):
        self.of["sync"] = f

    def gpsimd(self, f):
        self.of["gpsimd"] = f

    def scalar(self, f):
        self.of["scalar"] = f

    def vector(self, f):
        self.of["vector"] = f

    def tensor(self, f):
        self.of["tensor"] = f


def run(p, fast, general=None):

    def body(name):
        def both(e):
            f = fast.of.get(name)
            g = general.of.get(name) if general else None
            if not general:
                f(e)
                return
            asked = e.value_load(p.flag[0:1, 0:1], min_val=0, max_val=1)
            if f:
                with e.If(asked == 0):
                    f(e)
            if g:
                with e.If(asked == 1):
                    g(e)
        return both

    with p.nc.Block() as block:
        at = dict(sync=block.sync, gpsimd=block.gpsimd, scalar=block.scalar, vector=block.vector, tensor=block.tensor)
        for name, decorate in at.items():
            if name in fast.of or (general and name in general.of):
                decorate(body(name))
    p.end_stage()


class Serial:

    def __init__(self, p, steps, iterations):
        self.steps, self.iterations = steps, iterations
        self.done, self.dma, self.passed = p.sem("steps"), p.sem("gathered"), p.sem("passed")

    def body(self, e, me):
        if me == "vector":
            e.sem_inc(self.done)
        per = len(self.steps)
        with e.Fori(0, self.iterations) as i:
            for n, (engine, step) in enumerate(self.steps):
                if engine != me:
                    continue
                held(e, self.done, i * per + n + 1, self.passed)
                ins = step(e, i)
                if engine == "gpsimd":
                    ins.then_inc(self.dma, 16)
                    e.wait_ge(self.dma, i * 16 + 16)
                    e.sem_inc(self.done)
                else:
                    ins.then_inc(self.done, 1)
        e.wait_ge(self.done, self.iterations * per + 1)


def held(eng, sem, value, passed):
    eng.wait_ge(sem, value)
    eng.sem_inc(passed)


def bcast(ap, parts, at, n):
    return ap.rearrange("p (n o) -> p n o", o=1).to_broadcast([parts, n, at])


def prepare(p, t):
    nc, d = p.nc, p.d
    s_ld, s_io, s_ps = p.sem("loaded"), p.sem("iota"), p.sem("summed")
    s_sq = p.sem("sqrt")
    block = Bodies()

    @block.sync
    def _(e):
        e.dma_start(t.src, d["src_pt"][:, :]).then_inc(s_ld, 16)
        e.dma_start(t.dst, d["dst_pt"][:, :]).then_inc(s_ld, 16)
        e.dma_start(t.typ, d["typ_pt"][:, :]).then_inc(s_ld, 16)
        e.dma_start(t.gbase, d["gbase"].partition_broadcast(P)).then_inc(s_ld, 16)
        for k in range(3):
            e.dma_start(t.gains[:, k], d[f"g{k}"].partition_broadcast(P)).then_inc(s_ld, 16)
            e.dma_start(t.gains[:, 3 + k], d[f"beta{k}"].partition_broadcast(P)).then_inc(s_ld, 16)
            e.dma_start(t.sig[:, k:k + 1], d[f"a{k}"].partition_broadcast(P)).then_inc(s_ld, 16)
        e.wait_ge(s_ld, 13 * 16)

    @block.gpsimd
    def _(e):
        big = dict(allow_small_or_imprecise_dtypes=True)
        e.iota(t.iota_f, [[1, REL * WIN]], base=0, channel_multiplier=0, **big).then_inc(s_io, 1)
        e.iota(t.iota_h, [[1, BLOCKS * WIN]], base=0, channel_multiplier=0, **big).then_inc(s_io, 1)
        e.memset(p.ident[:, :], 0.0).then_inc(s_io, 1)
        e.wait_ge(s_io, 3)
        e.affine_select(out=p.ident[:, :], in_=p.ident[:, :], compare_op=ALU.not_equal, fill=1.0,
                        base=0, pattern=[[-1, P]], channel_multiplier=1).then_inc(s_io, 1)

    @block.vector
    def _(e):
        v = Tally(p.sem("prep"))
        e.wait_ge(s_ld, 13 * 16)
        v.inc(e.tensor_copy(t.typf, t.typ))
        v.inc(e.tensor_copy(t.dstf, t.dst))
        v.inc(e.tensor_copy(t.gbf, t.gbase))
        v.inc(e.tensor_scalar(t.shi, t.src, 7, None, ALU.arith_shift_right))
        v.inc(e.tensor_scalar(t.slo, t.src, P - 1, None, ALU.bitwise_and))
        v.inc(e.memset(t.bad, 0.0))
        v.inc(e.memset(t.ones, 1.0))
        v.inc(e.memset(p.small[:, 3:4], 1.0))
        v.link(e, e.memset(p.flag[:, :], 0))
        v.inc(e.tensor_copy(t.slof, t.slo))
        v.inc(e.tensor_copy(t.shif, t.shi))
        v.link(e, e.tensor_tensor(t.dloc.rearrange("p (g k) -> p g k", k=GT),
                                  t.dstf.rearrange("p (g k) -> p g k", k=GT),
                                  bcast(t.gbf, P, GT, GPAD), ALU.subtract))
        v.inc(e.scalar_tensor_tensor(t.keyf, t.shif, float(WIN), t.dloc, ALU.mult, ALU.add))
        full = t.dloc[:, 0:TILES - 1]
        v.inc(e.tensor_reduce(t.red[:, 0:1], full, AX.X, ALU.max))
        v.inc(e.tensor_reduce(t.red[:, 1:2], full, AX.X, ALU.min))
        groups = TILES // GT + 1
        v.inc(e.tensor_tensor(t.gdiff[:, 0:groups - 3], t.gbf[:, 3:groups], t.gbf[:, 0:groups - 3],
                              ALU.subtract))
        v.inc(e.tensor_reduce(t.red[:, 3:4], t.gains[:, 0:3], AX.XY, ALU.max, apply_absolute_value=True))
        v.link(e, e.tensor_reduce(t.red[:, 4:5], t.gains[:, 3:6], AX.XY, ALU.max, apply_absolute_value=True))
        v.inc(e.tensor_reduce(t.red[:, 2:3], t.gdiff[:, 0:groups - 3], AX.X, ALU.min))
        v.link(e, e.scalar_tensor_tensor(t.red[:, 6:7], t.red[:, 3:4], float(HID) ** 0.5, t.red[:, 4:5],
                                         ALU.mult, ALU.add))
        v.inc(e.tensor_scalar(t.bad[:, 0:1], t.red[:, 0:1], float(WIN - 1), None, ALU.is_gt))
        v.inc(e.tensor_scalar(t.bad[:, 1:2], t.red[:, 1:2], 0.0, None, ALU.is_lt))
        v.inc(e.tensor_scalar(t.bad[:, 2:3], t.red[:, 2:3], 0.0, None, ALU.is_le))
        v.inc(e.tensor_scalar(t.bad[:, 3:4], t.red[:, 6:7], F16_TOP / SCALE, None, ALU.is_gt))
        last = t.dloc[0:LAST, TILES - 1:TILES]
        v.inc(e.tensor_scalar(t.bad[0:LAST, 5:6], last, float(WIN - 1), None, ALU.is_gt))
        v.inc(e.tensor_scalar(t.bad[0:LAST, 6:7], last, 0.0, None, ALU.is_lt))
        e.wait_ge(v.sem, v.n)
        e.sem_inc(s_sq)
        e.wait_ge(s_ps, 1)
        v.link(e, e.tensor_reduce(t.red[0:1, 8:9], p.psum[0:1, 0, 0:8], AX.X, ALU.max))
        v.link(e, e.tensor_scalar(p.flag[:, :], t.red[0:1, 8:9], 0.0, None, ALU.is_gt))
        e.wait_ge(s_sq, 2)
        v.link(e, e.tensor_scalar(t.sig[:, 0:3], t.sig[:, 0:3], 1.0, None, ALU.add))
        v.link(e, e.reciprocal(p.small[:, 0:3], t.sig[:, 0:3]))

    @block.scalar
    def _(e):
        e.wait_ge(s_ld, 13 * 16)
        e.wait_ge(s_sq, 1)
        e.activation(t.sig[:, 0:3], t.sig[:, 0:3], ACT.Exp, scale=-1.0).then_inc(s_sq, 1)

    @block.tensor
    def _(e):
        e.wait_ge(s_sq, 1)
        e.matmul(p.psum[0:1, 0, 0:8], t.ones[:, 0:1], t.bad[:, :], start=True, stop=True).then_inc(s_ps, 1)
    return block


GW, NW = 400, NPAD // 400


def one_hot_of_dst(t, k):
    return "vector", lambda e, i: e.tensor_scalar(t.gen_oh, t.gen_iota, t.gen_dst[:, k:k + 1], None, ALU.is_equal)


def place_of_dst(t, column):
    return "vector", lambda e, i: e.tensor_tensor(
        t.gen_dst, column(i).to_broadcast([P, NW]), t.gen_starts, ALU.subtract)


def general_constants(p, t, block, s_go):
    @block.gpsimd
    def _(e):
        big = dict(allow_small_or_imprecise_dtypes=True)
        e.iota(t.gen_iota, [[1, GW]], base=0, channel_multiplier=0, **big).then_inc(s_go, 1)
        e.iota(t.gen_starts, [[GW, NW]], base=0, channel_multiplier=0, **big).then_inc(s_go, 1)


def count_relations_general(p, t):
    s_go = p.sem("constants")
    block = Bodies()
    general_constants(p, t, block, s_go)
    steps = [("vector", lambda e, i: e.tensor_tensor(
                  t.gen_rel, t.iota_f[:, 0:32], t.typf[:, bass.ds(i, 1)].to_broadcast([P, 32]), ALU.is_equal)),
             place_of_dst(t, lambda i: t.dstf[:, bass.ds(i, 1)])]
    for k in range(NW):
        at = t.cnt[:, k * GW:(k + 1) * GW]
        steps += [one_hot_of_dst(t, k),
                  ("tensor", lambda e, i: e.matmul(p.psum[0:32, 0, 0:GW], t.gen_rel, t.gen_oh, start=True, stop=True)),
                  ("vector", lambda e, i, at=at: e.tensor_tensor(at, at, p.psum[0:32, 0, 0:GW], ALU.add))]
    loop = Serial(p, steps, TPAD)
    s_z = p.sem("zeroed")

    @block.vector
    def _(e):
        e.wait_ge(s_go, 2)
        e.memset(t.cnt, 0.0).then_inc(s_z, 1)
        e.wait_ge(s_z, 1)
        loop.body(e, "vector")

    @block.tensor
    def _(e):
        loop.body(e, "tensor")
    return block


def edge_weights_general(p, t):
    nc, d = p.nc, p.d
    s_dg, s_sq, s_st = p.sem("degrees"), p.sem("root"), p.sem("stored")
    block = Bodies()
    steps = [("vector", lambda e, i: e.tensor_tensor(
                  t.gen_rel, t.iota_f[:, 0:32], t.typf[:, bass.ds(i, 1)].to_broadcast([P, 32]), ALU.is_equal)),
             ("tensor", lambda e, i: e.transpose(p.psum[0:32, 1, 0:P], t.gen_rel, p.ident[:, :])),
             ("vector", lambda e, i: e.tensor_copy(t.gen_relt, p.psum[0:32, 1, 0:P])),
             place_of_dst(t, lambda i: t.dstf[:, bass.ds(i, 1)])]
    for k in range(NW):
        steps += [one_hot_of_dst(t, k),
                  ("tensor", lambda e, i, k=k: e.matmul(p.psum[:, 0, 0:GW], t.gen_relt, t.cnt[:, k * GW:(k + 1) * GW],
                                                        start=True, stop=True)),
                  ("vector", lambda e, i: e.tensor_tensor(t.gen_oh, t.gen_oh, p.psum[:, 0, 0:GW], ALU.mult)),
                  ("vector", lambda e, i, k=k: e.tensor_reduce(t.gen_part[:, k:k + 1], t.gen_oh, AX.X, ALU.add))]
    steps += [("vector", lambda e, i: e.tensor_reduce(t.gen_sum, t.gen_part, AX.X, ALU.add)),
              ("vector", lambda e, i: e.tensor_copy(t.wgt[:, bass.ds(i, 1)], t.gen_sum))]
    loop = Serial(p, steps, TPAD)

    @block.sync
    def _(e):
        store_weights(e, p, t, s_dg, s_st)

    @block.vector
    def _(e):
        v = Tally(p.sem("tail"))
        loop.body(e, "vector")
        finish_weights(e, v, p, t, s_dg, s_sq)

    @block.scalar
    def _(e):
        root_of_degree(e, t, s_dg, s_sq)

    @block.tensor
    def _(e):
        sum_degrees(e, p, t, s_dg)
        loop.body(e, "tensor")
    return block


def store_weights(e, p, t, s_dg, s_st):
    e.wait_ge(s_dg, 2)
    e.dma_start(p.d["w_pt"][:, :], t.wgt).then_inc(s_st, 16)
    e.wait_ge(s_st, 16)


def finish_weights(e, v, p, t, s_dg, s_sq):
    v.link(e, e.tensor_scalar(t.wgt, t.wgt, 1.0, None, ALU.max))
    v.link(e, e.reciprocal(t.wgt, t.wgt))
    e.wait_ge(s_dg, 1)
    v.link(e, e.tensor_scalar(t.deg, p.psum[:, 7, 0:BLOCKS], 1.0, None, ALU.add))
    e.sem_inc(s_dg)
    e.wait_ge(s_sq, 1)
    inverse_root(v, e, t.degr, t.deg, t.degt)
    for k, f in ((1, SCALE), (3, 1 / SCALE)):
        v.inc(e.tensor_scalar(p.cols[:, k, :], t.degr, f, None, ALU.mult))
    e.wait_ge(v.sem, v.n)


def root_of_degree(e, t, s_dg, s_sq):
    e.wait_ge(s_dg, 2)
    e.activation(t.degr, t.deg, ACT.Sqrt).then_inc(s_sq, 1)


def sum_degrees(e, p, t, s_dg):
    for b in range(BLOCKS):
        m = e.matmul(p.psum[:, 7, b:b + 1], t.cnt[:, b * P:(b + 1) * P], t.ones[0:32, 0:1], start=True, stop=True)
    m.then_inc(s_dg, 1)


def count_relations(p, t):
    nc = p.nc
    G = CHUNK // GT
    ROUNDS = TPAD // CHUNK
    s_oh, s_cp, s_mm, s_ad, s_z = (p.sem(n) for n in ("onehots", "copied", "counted", "added", "zeroed"))
    passed = p.sem("passed")
    block = Bodies()

    @block.gpsimd
    def _(e):
        e.memset(t.cnt4, 0.0).then_inc(s_z, 1)
        e.wait_ge(s_z, 1)

    @block.vector
    def _(e):
        v = Tally(s_ad)
        regs = [e.alloc_register(f"cnt_base{k}") for k in range(G)]

        def onehots(r):
            e.tensor_tensor(t.all_r[:, bass.ds(r * CHUNK * 32, CHUNK * 32)].rearrange("p (t r) -> p t r", r=32),
                            t.iota_f[:, 0:32].rearrange("p (o r) -> p o r", o=1).to_broadcast([P, CHUNK, 32]),
                            bcast(t.typf[:, bass.ds(r * CHUNK, CHUNK)], P, 32, CHUNK), ALU.is_equal).then_inc(s_oh, 1)
            e.tensor_tensor(t.all_c[:, bass.ds(r * CHUNK * WIN, CHUNK * WIN)].rearrange("p (t w) -> p t w", w=WIN),
                            t.iota_f[:, 0:WIN].rearrange("p (o r) -> p o r", o=1).to_broadcast([P, CHUNK, WIN]),
                            bcast(t.dloc[:, bass.ds(r * CHUNK, CHUNK)], P, WIN, CHUNK), ALU.is_equal).then_inc(s_oh, 1)

        def adds(r, par):
            e.load(regs, t.gbase[0:1, bass.ds(r * G, G)])
            e.wait_ge(s_mm, r + 3)
            for g in range(G):
                base = e.snap(regs[g], min_val=0, max_val=NODES - 1)
                at = t.cnt[:, bass.ds(base, WIN)]
                v.link(e, e.tensor_tensor(at, at, p.psum[0:32, par, g * WIN:(g + 1) * WIN], ALU.add))

        onehots(0)
        e.sem_inc(s_ad, 2 * G - 1)
        v.n = 2 * G - 1
        v.link(e, e.memset(t.cnt, 0.0))
        with e.Fori(0, ROUNDS // 2) as i:
            v.enter(i, 2 * G)
            for par in range(2):
                onehots(i * 2 + par + 1)
                adds(i * 2 + par, par)
            v.leave(ROUNDS // 2)
        adds(ROUNDS - 1, 0)

    @block.scalar
    def _(e):
        def copy(r, par):
            held(e, s_oh, r * 2 + 2, passed)
            held(e, s_mm, r + 1, passed)
            e.activation(t.now_r[par], t.all_r[:, bass.ds(r * CHUNK * 32, CHUNK * 32)], ACT.Copy).then_inc(s_cp, 1)
            e.activation(t.now_c[par], t.all_c[:, bass.ds(r * CHUNK * WIN, CHUNK * WIN)], ACT.Copy).then_inc(s_cp, 1)

        with e.Fori(0, ROUNDS // 2) as i:
            for par in range(2):
                copy(i * 2 + par, par)
        copy(ROUNDS - 1, 0)

    @block.tensor
    def _(e):
        e.sem_inc(s_mm, 2)

        def count(r, par):
            e.wait_ge(s_cp, r * 2 + 2)
            e.wait_ge(s_ad, r * G + G)
            for k in range(CHUNK):
                g = k // GT
                m = e.matmul(p.psum[0:32, par, g * WIN:(g + 1) * WIN], t.now_r[par][:, k * 32:(k + 1) * 32],
                             t.now_c[par][:, k * WIN:(k + 1) * WIN], start=(k % GT == 0), stop=(k % GT == GT - 1))
            m.then_inc(s_mm, 1)

        with e.Fori(0, ROUNDS // 2) as i:
            for par in range(2):
                count(i * 2 + par, par)
        count(ROUNDS - 1, 0)
    return block


def edge_weights(p, t):
    nc, d = p.nc, p.d
    PER = 16
    G = PER // GT
    ROUNDS = TPAD // PER
    SPREAD = -(-NPAD // 512)
    TURNED, FETCHED = 0, 2
    s_pr, s_sp, s_cp, s_tr, s_tv, s_mm, s_oh, s_dg, s_sq, s_st = (p.sem(n) for n in (
        "prepared", "spread", "counts", "turned", "relations", "fetched", "selected", "degrees", "root", "stored"))
    passed = p.sem("passed")
    block = Bodies()

    def planes(k0):
        return [(g, min(512, NPAD - 512 * g), k, t.cnt4[32 * k:32 * k + 32, k, g * 512:min(NPAD, g * 512 + 512)])
                for g in range(SPREAD) for k in (k0, k0 + 1)]

    @block.sync
    def _(e):
        store_weights(e, p, t, s_dg, s_st)

    @block.vector
    def _(e):
        e.tensor_copy(t.rep.rearrange("p (k r) -> p k r", k=GT),
                      p.ident[0:32, 0:32].rearrange("p (o r) -> p o r", o=1).to_broadcast([32, GT, 32])).then_inc(s_pr, 1)
        e.tensor_copy(t.ident_h, p.ident[:, :]).then_inc(s_pr, 1)
        v = Tally(s_oh)
        for g, n, k, at in planes(0):
            e.wait_ge(s_sp, g + 1)
            e.tensor_copy(at, p.psum[32 * k:32 * k + 32, g, 0:n]).then_inc(s_cp, 1)
        e.sem_inc(s_oh, 4)
        v.n = 4

        def select(r, par):
            e.wait_ge(s_mm, r + 3)
            v.link(e, e.tensor_tensor(t.picked[par], t.all_c[:, bass.ds(r * PER * WIN, PER * WIN)],
                                      p.psum[:, FETCHED + par, 0:PER * WIN], ALU.mult))
            v.inc(e.tensor_reduce(t.wgt[:, bass.ds(r * PER, PER)],
                                  t.picked[par].rearrange("p (t w) -> p t w", w=WIN), AX.X, ALU.add))

        with e.Fori(0, ROUNDS // 2) as i:
            v.enter(i, 4)
            for par in range(2):
                select(i * 2 + par, par)
                e.wait_ge(s_oh, v.now())
            v.leave(ROUNDS // 2)
        select(ROUNDS - 1, 0)
        e.wait_ge(s_oh, v.now())
        finish_weights(e, v, p, t, s_dg, s_sq)

    @block.scalar
    def _(e):
        for g, n, k, at in planes(2):
            e.wait_ge(s_sp, g + 1)
            e.activation(at, p.psum[32 * k:32 * k + 32, g, 0:n], ACT.Copy).then_inc(s_cp, 1)
        e.sem_inc(s_tv, 2)

        def take(r, par):
            held(e, s_tr, r + 1, passed)
            held(e, s_mm, r + 1, passed)
            e.activation(t.turned[par], p.psum[:, TURNED + par, :], ACT.Copy).then_inc(s_tv, 1)

        with e.Fori(0, ROUNDS // 2) as i:
            for par in range(2):
                take(i * 2 + par, par)
        take(ROUNDS - 1, 0)
        root_of_degree(e, t, s_dg, s_sq)

    @block.tensor
    def _(e):
        sum_degrees(e, p, t, s_dg)
        e.wait_ge(s_pr, 2)
        for g in range(SPREAD):
            n = min(512, NPAD - 512 * g)
            e.matmul(p.psum[:, g, 0:n], t.rep, t.cnt[:, g * 512:g * 512 + n], start=True, stop=True).then_inc(s_sp, 1)
        e.wait_ge(s_cp, GT * SPREAD)
        e.sem_inc(s_mm, 2)
        regs = [e.alloc_register(f"w_base{k}") for k in range(2 * G)]

        def turn(r, par):
            e.wait_ge(s_tv, r + 1)
            for g in range(G):
                m = e.matmul(p.psum[:, TURNED + par, g * P:(g + 1) * P],
                             t.all_r[:, bass.ds(r * PER * 32 + g * P, P)], t.ident_h, start=True, stop=True)
            m.then_inc(s_tr, 1)

        def fetch(r, par):
            e.wait_ge(s_tv, r + 3)
            e.wait_ge(s_oh, r * 2 + 1)
            for g in range(G):
                base = e.snap(regs[par * G + g], min_val=0, max_val=NODES - 1)
                m = e.matmul(p.psum[:, FETCHED + par, g * GT * WIN:(g + 1) * GT * WIN],
                             t.turned[par][:, g * P:(g + 1) * P], t.cnt4[:, :, bass.ds(base, WIN)],
                             start=True, stop=True)
            m.then_inc(s_mm, 1)

        turn(0, 0)
        with e.Fori(0, ROUNDS // 2) as i:
            e.load(regs, t.gbase[0:1, bass.ds(i * 2 * G, 2 * G)])
            for par in range(2):
                turn(i * 2 + par + 1, 1 - par)
                fetch(i * 2 + par, par)
        e.load(regs[0:G], t.gbase[0:1, (ROUNDS - 1) * G:ROUNDS * G])
        fetch(ROUNDS - 1, 0)
    return block


def inverse_root(v, e, out, value, tmp):
    v.link(e, e.reciprocal(out, out))
    v.link(e, e.tensor_tensor(tmp, out, out, ALU.mult))
    v.link(e, e.tensor_tensor(tmp, tmp, value, ALU.mult))
    v.link(e, e.tensor_scalar(tmp, tmp, -0.5, 1.5, ALU.mult, ALU.add))
    v.link(e, e.tensor_tensor(out, out, tmp, ALU.mult))


def moments(v, e, x, stats, mv, n, passed):
    for k in range(n):
        v.inc(e.bn_stats(stats[:, k, :], x[:, k, :]))
    held(e, v.sem, v.now(), passed)
    for k in range(n):
        v.inc(e.bn_aggr(mv[:, k, :], stats[:, k, :]))
    e.wait_ge(v.sem, v.now())


ZEROED = 16


def zero_adjacency(e, p, b0, b1):
    return e.memset(p.arena[:, b0 * NPAD:b1 * NPAD].bitcast(F32), 0.0)


def first_norm(p, t, fast):
    nc, d = p.nc, p.d
    s_ld, s_v, s_sq, s_st = p.sem("x"), p.sem("norm"), p.sem("roots"), p.sem("stored")
    whole = (BLOCKS - 1) * P
    block = Bodies()

    if fast:
        @block.gpsimd
        def _(e):
            s_z = p.sem("zeroed")
            zero_adjacency(e, p, 0, ZEROED).then_inc(s_z, 1)
            e.wait_ge(s_z, 1)

    @block.sync
    def _(e):
        e.dma_start(t.x[:, 0:BLOCKS - 1, :], d["x"][0:whole, :].rearrange("(b p) f -> p b f", p=P)).then_inc(s_ld, 16)
        e.wait_ge(s_v, 1)
        e.dma_start(t.x[0:NODES - whole, BLOCKS - 1, :], d["x"][whole:NODES, :]).then_inc(s_ld, 16)
        e.wait_ge(s_sq, 3)
        e.dma_start(d["x_pad"].rearrange("(b p) f -> p b f", p=P), t.x).then_inc(s_st, 16)
        e.dma_start(d["h16_0"].rearrange("(b p) h f -> p b (h f)", p=P),
                    t.h0[:, :, :, :].rearrange("p b h f -> p b (h f)")).then_inc(s_st, 16)
        e.wait_ge(s_st, 32)

    @block.vector
    def _(e):
        v = Tally(s_v)
        v.inc(e.memset(t.x[:, BLOCKS - 1, :], 0.0))
        e.wait_ge(s_ld, 32)
        moments(v, e, t.x, t.stats, t.mv, BLOCKS, p.sem("passed"))
        v.link(e, e.tensor_scalar(t.var, t.mv[:, :, 1], EPS, None, ALU.add))
        e.sem_inc(s_sq)
        e.wait_ge(s_sq, 2)
        inverse_root(v, e, t.rstd, t.var, t.tmp)
        v.link(e, e.tensor_tensor(t.rstd, t.rstd, p.cols[:, 1, :], ALU.mult))
        for b in range(BLOCKS):
            v.inc(e.tensor_scalar(t.y[:, b, :], t.x[:, b, :], t.mv[:, b, 0:1], t.rstd[:, b:b + 1],
                                  ALU.subtract, ALU.mult))
        e.wait_ge(s_v, v.n)
        v.link(e, e.tensor_scalar(t.h0[:, :, 0, :], t.y, 0.0, None, ALU.max))
        v.link(e, e.scalar_tensor_tensor(t.h0[:, :, 1, :], t.y, 0.0, t.h0[:, :, 0, :], ALU.max, ALU.subtract))
        e.sem_inc(s_sq)

    @block.scalar
    def _(e):
        e.wait_ge(s_sq, 1)
        e.activation(t.rstd, t.var, ACT.Sqrt).then_inc(s_sq, 1)
    return block


def norm_memory(p):
    t = Bag()
    c = p.carve(26000)
    t.x = c(BLOCKS * RF).rearrange("p (b f) -> p b f", b=BLOCKS)
    t.y = c(BLOCKS * RF).rearrange("p (b f) -> p b f", b=BLOCKS)
    t.h0 = c(BLOCKS * RF, F16).rearrange("p (b h f) -> p b h f", b=BLOCKS, h=2)
    t.stats = c(BLOCKS * 6).rearrange("p (b s) -> p b s", b=BLOCKS)
    t.mv = c(BLOCKS * 2).rearrange("p (b s) -> p b s", b=BLOCKS)
    t.var, t.rstd, t.tmp = c(BLOCKS), c(BLOCKS), c(BLOCKS)
    return t


AT = 8
ASCAL = 7
NKEY = AT + AT - ASCAL


def adjacency_memory(p, t):
    h = p.h16[:, :, :, :].rearrange("p a b c -> p (a b c)").bitcast(F32)
    w = p.work[:, :]
    n = AT * BLOCKS * WIN // 2
    m = AT * P // 2
    t.slof, t.keyf = h[:, 0:TPAD], h[:, TPAD:2 * TPAD]
    at = 2 * TPAD
    t.iota_h = h[:, at:at + BLOCKS * WIN // 2].bitcast(F16)
    at += BLOCKS * WIN // 2
    t.columns = h[:, 0:2 * TPAD].rearrange("p (c n) -> p c n", c=2)
    t.stage = h[:, at:at + 4 * AT].rearrange("p (r c k) -> p r c k", r=2, c=2)
    at += 4 * AT
    t.gbase = w[:, 0:GPAD].bitcast(I32)
    t.oh_k = [h[:, at:at + n], w[:, GPAD:GPAD + n]]
    at += n
    t.oh_s = [w[:, GPAD + n:GPAD + n + m], w[:, GPAD + n + m:GPAD + n + 2 * m]]
    rest = GPAD + n + 2 * m
    t.away = w[:, rest:rest + ASCAL * P // 2].bitcast(F16).rearrange("p (k n) -> p k n", k=ASCAL)
    rest += ASCAL * P // 2
    c = BLOCKS * WIN // 2
    t.counts = [h[:, at + k * c:at + (k + 1) * c] for k in range(2)] + [
        w[:, rest + k * c:rest + (k + 1) * c] for k in range(2)]
    assert at + 2 * c <= BLOCKS * HID and rest + 2 * c <= 8 * GN, (at, rest)
    t.oh_k = [a.bitcast(F16).rearrange("p (k n) -> p k n", k=AT) for a in t.oh_k]
    t.oh_s = [a.bitcast(F16).rearrange("p (k n) -> p k n", k=AT) for a in t.oh_s]
    t.counts = [a.bitcast(F16) for a in t.counts]


def build_adjacency(p, t):
    G = AT // GT
    ROUNDS = EDGE_TILES // AT
    HALF = BLOCKS * WIN // 2
    adj = p.arena[:, :].rearrange("p (b n) -> p b n", b=BLOCKS)
    s_z, s_src, s_key, s_mm, s_ct, s_ad, s_st, s_df = (p.sem(n) for n in (
        "zeroed", "sources", "keys", "outer", "counts", "added", "staged", "away"))
    passed = p.sem("passed")
    block = Bodies()

    @block.gpsimd
    def _(e):
        zero_adjacency(e, p, ZEROED, ZEROED + 3).then_inc(s_z, 1)

    @block.vector
    def _(e):
        v = Tally(s_ad)
        zero_adjacency(e, p, ZEROED + 3, BLOCKS).then_inc(s_z, 1)
        e.wait_ge(s_z, 2)
        for b in range(BLOCKS):
            v.inc(e.tensor_copy(adj[:, b, b * P:(b + 1) * P], p.ident[:, :]))
        e.wait_ge(s_ad, v.n)
        n0 = v.n
        regs = [e.alloc_register(f"adj_base{k}") for k in range(2 * G)]
        e.sem_inc(s_st)

        def keys(r, par):
            e.wait_ge(s_key, r * NKEY + 1)
            e.wait_ge(s_src, r + 1)
            e.tensor_copy(t.stage[:, par, :, :], t.columns[:, :, bass.ds(r * AT, AT)]).then_inc(s_st, 1)
            e.wait_ge(s_st, r + 2)
            e.wait_ge(s_mm, r * G + 1)
            for k in range(AT):
                e.tensor_scalar(t.oh_k[par][:, k, :], t.iota_h, t.stage[:, par, 1, k:k + 1], None,
                                ALU.is_equal).then_inc(s_key, 1)
                if k >= ASCAL:
                    e.tensor_scalar(t.oh_s[par][:, k, :], t.iota_h[:, 0:P], t.stage[:, par, 0, k:k + 1], None,
                                    ALU.is_equal).then_inc(s_key, 1)

        def adds(r, par, before):
            for g in range(G):
                base = e.snap(regs[par * G + g], min_val=0, max_val=NODES - 1)
                e.wait_ge(s_ct, r * G + g + 2 * G + 1)
                at = adj[:, :, bass.ds(base, WIN)]
                e.tensor_tensor(at, t.counts[par * G + g].rearrange("p (b w) -> p b w", b=BLOCKS), at, ALU.add).then_inc(s_ad, 1)
                e.wait_ge(s_ad, before + g + 1)

        e.sem_inc(s_key)
        keys(0, 0)
        keys(1, 1)
        with e.Fori(0, (ROUNDS - 3) // 2) as i:
            for par in range(2):
                r = i * 2 + par
                keys(r + 2, par)
                if par == 0:
                    e.load(regs, t.gbase[0:1, bass.ds(i * 2 * G, 2 * G)])
                adds(r, par, r * G + n0)
        for r in range(ROUNDS - 3, ROUNDS):
            if r % 2 == 0:
                n = min(2 * G, GPAD - r * G)
                e.load(regs[0:n], t.gbase[0:1, r * G:r * G + n])
            if r + 2 < ROUNDS:
                keys(r + 2, r % 2)
            adds(r, r % 2, r * G + n0)

    @block.scalar
    def _(e):
        e.sem_inc(s_ct, 2 * G)
        e.sem_inc(s_src, 2)

        def sources(r, par):
            held(e, s_st, r + 2, passed)
            held(e, s_src, r + 2, passed)
            for k in range(ASCAL):
                e.activation(t.away[:, k, :], t.iota_h[:, 0:P], ACT.Abs, bias=t.stage[:, par, 0, k:k + 1],
                             scale=-1.0).then_inc(s_df, 1)
            held(e, s_mm, r * G + 1, passed)
            held(e, s_df, r * ASCAL + ASCAL, passed)
            e.activation(t.oh_s[par][:, 0:ASCAL, :], t.away, ACT.Relu, bias=p.small[:, 3:4],
                         scale=-1.0).then_inc(s_src, 1)

        def take(r, par):
            for g in range(G):
                held(e, s_mm, r * G + g + G + 2, passed)
                held(e, s_ad, r * G + g + BLOCKS + 1 - 2 * G, passed)
                e.activation(t.counts[par * G + g].rearrange("p (a n) -> p a n", a=2),
                             p.psum[:, 4 * par + 2 * g:4 * par + 2 * g + 2, 0:HALF], ACT.Copy).then_inc(s_ct, 1)

        sources(0, 0)
        sources(1, 1)
        with e.Fori(0, (ROUNDS - 3) // 2) as i:
            for par in range(2):
                r = i * 2 + par
                take(r, par)
                sources(r + 2, par)
        for r in range(ROUNDS - 3, ROUNDS):
            take(r, r % 2)
            if r + 2 < ROUNDS:
                sources(r + 2, r % 2)

    @block.tensor
    def _(e):
        e.sem_inc(s_mm, G + 1)

        def turn(r, par):
            for g in range(G):
                upto = (g + 1) * GT
                e.wait_ge(s_src, r + 3)
                e.wait_ge(s_key, r * NKEY + upto + max(0, upto - ASCAL) + 1)
                e.wait_ge(s_ct, r * G + g + 1)
                for k in range(g * GT, g * GT + GT):
                    for half in range(2):
                        m = e.matmul(p.psum[:, 4 * par + 2 * g + half, 0:HALF], t.oh_s[par][:, k, :],
                                     t.oh_k[par][:, k, half * HALF:(half + 1) * HALF],
                                     start=(k % GT == 0), stop=(k % GT == GT - 1))
                m.then_inc(s_mm, 1)

        with e.Fori(0, ROUNDS // 2) as i:
            for par in range(2):
                turn(i * 2 + par, par)
        turn(ROUNDS - 1, 0)
    return block


GB = 5
GROUPS = BLOCKS // GB
GN = GB * P


def general_gcn_memory(p):
    t = Bag()
    edges = edge_columns(p)
    t.src, t.dstf = edges.src, edges.dstf
    c = p.carve(26000)
    t.sums = c(2 * NPAD).rearrange("p (k n) -> p k n", k=2)
    t.gen_idx, t.gen_to, t.gen_nodes = c(TPAD + BLOCKS, I32), c(TPAD + BLOCKS), c(BLOCKS, I32)
    t.gen_oh, t.gen_iota, t.gen_dst, t.gen_starts = c(GW), c(GW), c(NW), c(NW)
    t.pick, t.halves, t.row = c(1, I32), c(HID, F16), c(HID)
    return t


def general_aggregate(p, t, l, kh):
    fin = kh * P
    steps = [("vector", lambda e, i: e.tensor_copy(t.pick, t.gen_idx[:, bass.ds(i, 1)])),
             ("gpsimd", lambda e, i: e.indirect_dma_start(
                 out=t.halves[:, 0:2 * fin], out_offset=None, in_=p.d[f"h16_{l}"].rearrange("n h f -> n (h f)"),
                 in_offset=bass.IndirectOffsetOnAxis(ap=t.pick, axis=0))),
             ("vector", lambda e, i: e.tensor_tensor(t.row[:, 0:fin], t.halves[:, 0:fin], t.halves[:, fin:2 * fin],
                                                     ALU.add)),
             place_of_dst(t, lambda i: t.gen_to[:, bass.ds(i, 1)])]
    for k in range(NW):
        steps.append(one_hot_of_dst(t, k))
        for f in range(kh):
            at = t.sums[:, f, k * GW:(k + 1) * GW]
            steps += [("tensor", lambda e, i, f=f: e.matmul(p.psum[:, 0, 0:GW], t.row[:, f * P:(f + 1) * P], t.gen_oh,
                                                            start=True, stop=True)),
                      ("vector", lambda e, i, at=at: e.tensor_tensor(at, at, p.psum[:, 0, 0:GW], ALU.add))]
    return Serial(p, steps, TPAD + BLOCKS)


def load_input(e, p, l, q):
    f = 2 * (RF if l == 0 else HID)
    h = p.h16[:, :, :, :].rearrange("p b h f -> p (b h f)")[:, 0:BLOCKS * f].rearrange("p (b f) -> p b f", b=BLOCKS)
    return e.dma_start(h[:, q * GB:q * GB + GB],
                       p.d[f"h16_{l}"][q * GN:q * GN + GN].rearrange("(b p) h f -> p b (h f)", p=P))


def gcn_layers(p, fast):
    done, layers = None, []
    for l in range(4):
        layer, done = gcn_layer(p, l, fast, done)
        layers.append(layer)
    block = Bodies()
    for name in layers[0].of:
        def body(e, name=name):
            for layer in layers:
                layer.of[name](e)
        block.of[name] = body
    return block


def gcn_layer(p, l, fast, before):
    nc, d = p.nc, p.d
    last = l == 3
    fin, fout = (RF if l == 0 else HID), (RF if last else HID)
    KH = fin // P
    h = p.h16[:, :, :, :].rearrange("p b h f -> p (b h f)")[:, 0:BLOCKS * 2 * fin].rearrange(
        "p (b h f) -> p b h f", b=BLOCKS, h=2)
    adj = p.arena[:, :].rearrange("p (b n) -> p b n", b=BLOCKS)
    work = p.work[:, :]
    zt = work[:, 0:2 * GN].rearrange("p (k n) -> p k n", k=2)
    u = work[:, 2 * GN:2 * GN + GB * fout].rearrange("p (b f) -> p b f", b=GB)
    ex = work[:, 4 * GN:4 * GN + GB * fout].rearrange("p (b f) -> p b f", b=GB)
    ho = work[:, 6 * GN:8 * GN].bitcast(F16).rearrange("p (b h f) -> p b h f", b=GB, h=2)
    xg = work[:, 6 * GN:7 * GN].rearrange("p (b f) -> p b f", b=GB)
    brow, gain, shift = (p.rows[:, k, 0:fout] for k in range(3))
    over = [r.rearrange("p (o f) -> p o f", o=1).to_broadcast([P, GB, fout]) for r in (gain, shift)]
    ln = p.lnbuf
    stats = ln[:, 0:6 * GB].rearrange("p (b s) -> p b s", b=GB)
    mv = ln[:, 30:40].rearrange("p (b s) -> p b s", b=GB)
    var, rstd, tmp, cs, ds = ln[:, 40:45], ln[:, 45:50], ln[:, 50:55], ln[:, 55:60], ln[:, 60:65]
    csig = p.csig[:, :]
    bank = p.psum[:, :, :].rearrange("p a b -> p (a b)")
    s_w, s_mm, s_v, s_a, s_vq, s_st, s_x = (p.sem(n) for n in (
        "weights", "products", "node_ops", "scalar_ops", "asked", "stored", "x"))
    s_next = [p.sem("next_inputs") for _ in range(GROUPS - 1)]
    s_in = (before.inputs if before else [p.sem("inputs") for _ in range(GROUPS - 1)]) + [p.sem("last_input")]
    passed = p.sem("passed")
    NM, NA = KH + 1, KH + (1 if last else 2)

    loop = t = None
    if not fast:
        t = general_gcn_memory(p)
        loop, s_go = general_aggregate(p, t, l, KH), p.sem("constants")
    block = Bodies()

    @block.sync
    def _(e):
        if before is None:
            for q in range(GROUPS - 1):
                load_input(e, p, l, q).then_inc(s_in[q], 16)
        else:
            e.wait_ge(*before.products)
        e.dma_start(p.wts[:, 0:KH, 0:fout], d[f"W{l}"].rearrange("(k p) o -> p k o", p=P)).then_inc(s_w, 16)
        e.dma_start(brow, d[f"b{l}"].partition_broadcast(P)).then_inc(s_w, 16)
        if not last:
            e.dma_start(gain, d[f"g{l}"].partition_broadcast(P)).then_inc(s_w, 16)
            e.dma_start(shift, d[f"beta{l}"].partition_broadcast(P)).then_inc(s_w, 16)
        with e.Fori(0, GROUPS) as i:
            rows = bass.ds(i * GN, GN)
            if last:
                e.wait_ge(s_st, i * 32 + 16)
                e.dma_start(xg, d["x_pad"][rows, :].rearrange("(b p) f -> p b f", p=P)).then_inc(s_x, 16)
                e.wait_ge(s_vq, i * 4 + 3)
                e.dma_start(d["x1"][rows, :].rearrange("(b p) f -> p b f", p=P), u).then_inc(s_st, 16)
                e.wait_ge(s_vq, i * 4 + 5)
                e.dma_start(d["rows_0"][rows, :].rearrange("(b p) f -> p b f", p=P), ex).then_inc(s_st, 16)
            else:
                e.wait_ge(s_vq, i * 4 + 5)
                e.dma_start(d[f"h16_{l + 1}"][rows].rearrange("(b p) h f -> p b (h f)", p=P),
                            ho.rearrange("p b h f -> p b (h f)")).then_inc(s_st, 16)
        e.wait_ge(s_st, 16 + GROUPS * (32 if last else 16))

    @block.gpsimd
    def _(e):
        if before:
            e.wait_ge(*before.stores)
        load_input(e, p, l, GROUPS - 1).then_inc(s_in[-1], 16)
        e.sem_inc(s_st, 16)
        e.wait_ge(s_in[-1], 16)
        if not fast:
            big = dict(allow_small_or_imprecise_dtypes=True)
            e.iota(t.gen_iota, [[1, GW]], base=0, channel_multiplier=0, **big).then_inc(s_go, 1)
            e.iota(t.gen_starts, [[GW, NW]], base=0, channel_multiplier=0, **big).then_inc(s_go, 1)
            e.iota(t.gen_nodes, [[P, BLOCKS]], base=0, channel_multiplier=1).then_inc(s_go, 1)
            loop.body(e, "gpsimd")
        if not last:
            e.wait_ge(s_mm, (GROUPS - 1) * NM + KH + 1)
            for q in range(GROUPS - 1):
                e.wait_ge(s_st, 16 + (q + 1) * 16)
                load_input(e, p, l + 1, q).then_inc(s_next[q], 16)
            for q in range(GROUPS - 1):
                e.wait_ge(s_next[q], 16)

    @block.tensor
    def _(e):
        e.sem_inc(s_mm)
        e.sem_inc(s_a, NA)
        if not fast:
            loop.body(e, "tensor")
        nc.disable_value_cache = True
        with e.Fori(0, GROUPS) as i:
            if not fast:
                e.wait_ge(s_vq, i * 4 + 1)
                e.sem_inc(s_mm, KH)
            else:
                for q in range(GROUPS):
                    e.wait_ge(s_in[q], 16)
                    for k in range(KH):
                        if q == 0:
                            e.wait_ge(s_a, i * NA + k + 1)
                        for b in range(q * GB, q * GB + GB):
                            for half in range(2):
                                a, z = (b == 0 and half == 0), (b == BLOCKS - 1 and half == 1)
                                wt = h[:, b, half, k * P:(k + 1) * P]
                                e.matmul(bank[:, 1024 * k:1024 * k + 512], wt, adj[:, b, bass.ds(i * GN, 512)],
                                         start=a, stop=z)
                                m = e.matmul(bank[:, 1024 * k + 512:1024 * k + GN], wt,
                                             adj[:, b, bass.ds(i * GN + 512, GN - 512)], start=a, stop=z)
                        if q == GROUPS - 1:
                            m.then_inc(s_mm, 1)
            e.wait_ge(s_w, 16 * (2 if last else 4))
            e.wait_ge(s_a, i * NA + NA + KH)
            e.wait_ge(s_vq, i * 4 + 1)
            for b in range(GB):
                for k in range(KH):
                    m = e.matmul(bank[:, 2048 + b * 256:2048 + b * 256 + fout], zt[:, k, b * P:(b + 1) * P],
                                 p.wts[:, k, 0:fout], start=(k == 0), stop=(k == KH - 1))
            m.then_inc(s_mm, 1)
        nc.disable_value_cache = False

    @block.scalar
    def _(e):
        if not fast:
            e.wait_ge(loop.done, loop.iterations * len(loop.steps) + 1)
        with e.Fori(0, GROUPS) as i:
            held(e, s_mm, i * NM + 1, passed)
            for k in range(KH):
                held(e, s_mm, i * NM + k + 2, passed)
                got = bank[:, 1024 * k:1024 * k + GN] if fast else t.sums[:, k, bass.ds(i * GN, GN)]
                e.activation(zt[:, k, :], got, ACT.Copy).then_inc(s_a, 1)
            held(e, s_vq, i * 4 + 3, passed)
            e.activation(rstd, var, ACT.Sqrt).then_inc(s_a, 1)
            if not last:
                held(e, s_vq, i * 4 + 4, passed)
                e.activation(ex, ex, ACT.Exp).then_inc(s_a, 1)

    @block.vector
    def _(e):
        v = Tally(s_v)
        if before:
            e.wait_ge(*before.stores)
        if not fast:
            e.wait_ge(s_go, 3)
            v.inc(e.memset(t.sums, 0.0))
            v.inc(e.tensor_copy(t.gen_idx[:, 0:TPAD], t.src))
            v.inc(e.tensor_copy(t.gen_idx[:, TPAD:], t.gen_nodes))
            v.inc(e.tensor_copy(t.gen_to[:, 0:TPAD], t.dstf))
            v.link(e, e.tensor_copy(t.gen_to[:, TPAD:], t.gen_nodes))
            loop.body(e, "vector")
        e.wait_ge(s_w, 16 * (2 if last else 4))
        if last:
            v.link(e, e.tensor_copy(csig, p.cols[:, 3, :]))
        else:
            v.inc(e.tensor_scalar(csig, p.cols[:, 3, :], p.small[:, l:l + 1], None, ALU.mult))
            v.link(e, e.tensor_scalar(brow, brow, p.small[:, l:l + 1], None, ALU.mult))
        e.sem_inc(s_vq)
        per = (2 + GB + 1 + 2 * GB + 1 + 5 + GB + 1) if last else (2 + GB + 2 * GB + 1 + 5 + GB + 4 + GB + 2)
        with e.Fori(0, GROUPS) as i:
            v.enter(i, per)
            if not last:
                e.wait_ge(s_st, i * 16 + 16)
            else:
                e.wait_ge(s_st, i * 32 + 16)
            v.inc(e.tensor_copy(cs, csig[:, bass.ds(i * GB, GB)]))
            v.link(e, e.tensor_copy(ds, p.cols[:, 1, bass.ds(i * GB, GB)]))
            e.wait_ge(s_mm, i * NM + NM + 1)
            for b in range(GB):
                v.inc(e.scalar_tensor_tensor(u[:, b, :], bank[:, 2048 + b * 256:2048 + b * 256 + fout],
                                             cs[:, b:b + 1], brow, ALU.mult, ALU.add))
            e.wait_ge(s_v, v.now())
            e.sem_inc(s_vq)
            if last:
                e.wait_ge(s_x, i * 16 + 16)
                v.link(e, e.tensor_tensor(u, u, xg, ALU.add))
            moments(v, e, u, stats, mv, GB, passed)
            v.link(e, e.tensor_scalar(var, mv[:, :, 1], EPS, None, ALU.add))
            e.sem_inc(s_vq)
            e.wait_ge(s_a, i * NA + NA + KH + 1)
            inverse_root(v, e, rstd, var, tmp)
            to = ex if last else u
            for b in range(GB):
                v.inc(e.tensor_scalar(to[:, b, :], u[:, b, :], mv[:, b, 0:1], rstd[:, b:b + 1],
                                      ALU.subtract, ALU.mult))
            e.wait_ge(s_v, v.now())
            if last:
                e.sem_inc(s_vq)
                v.link(e, e.tensor_scalar(ex, ex, 0.0, None, ALU.max))
                e.sem_inc(s_vq)
            else:
                v.link(e, e.tensor_tensor(u, u, over[0], ALU.mult))
                v.link(e, e.tensor_tensor(u, u, over[1], ALU.add))
                v.link(e, e.tensor_scalar(ex, u, 0.0, None, ALU.min))
                e.sem_inc(s_vq)
                e.wait_ge(s_a, i * NA + NA + KH + 2)
                v.link(e, e.scalar_tensor_tensor(u, u, 0.0, ex, ALU.max, ALU.add))
                for b in range(GB):
                    v.inc(e.tensor_scalar(ex[:, b, :], u[:, b, :], -1.0, ds[:, b:b + 1], ALU.add, ALU.mult))
                e.wait_ge(s_v, v.now())
                v.link(e, e.tensor_copy(ho[:, :, 0, :], ex))
                v.link(e, e.tensor_tensor(ho[:, :, 1, :], ex, ho[:, :, 0, :], ALU.subtract))
                e.sem_inc(s_vq)
            v.leave(GROUPS)

    done = Bag()
    done.products = s_mm, 1 + GROUPS * NM
    done.stores = s_st, 16 + GROUPS * 16
    done.inputs = s_next
    return block, done


ROUND = 16


def relation_memory(p):
    t = Bag()
    c = p.carve(0)
    t.hrows = c(NPAD).rearrange("p (b f) -> p b f", b=BLOCKS)
    t.ht, t.acc = c(NPAD), c(NPAD)
    t.wr = c(REL * RF).rearrange("p (r o) -> p r o", r=REL)
    t.root, t.bias = c(RF), c(1)
    t.idx, t.rels, t.dsti = c(EDGE_TILES, I32), c(EDGE_TILES, I32), c(EDGE_TILES, I32)
    t.gbase = c(GPAD, I32)
    t.typf, t.dstf, t.gbf = c(EDGE_TILES), c(EDGE_TILES), c(GPAD)
    t.edge2 = c(2 * EDGE_TILES).rearrange("p (a t) -> p a t", a=2)
    t.iota = c(REL * WIN)
    t.stage = c(2 * ROUND)
    t.oh = c(ROUND * REL * WIN).rearrange("p (k n) -> p k n", k=ROUND)
    t.msg = c(ROUND * RF).rearrange("p (k n) -> p k n", k=ROUND)
    t.pick = c(ROUND, I32)
    t.agg = c(REL * ROUND // GT * WIN).rearrange("p (r g w) -> p r g w", r=REL, g=ROUND // GT)
    t.gen_oh, t.gen_iota, t.gen_dst, t.gen_starts = c(GW), c(GW), c(NW), c(NW)
    t.gen_rel, t.gen_types, t.gen_to, t.gen_y = c(REL), c(EDGE_TILES), c(EDGE_TILES), c(REL * RF)
    t.x1 = c(NPAD).rearrange("p (b f) -> p b f", b=BLOCKS)
    return t


def relation_setup(p, t):
    nc, d = p.nc, p.d
    s_ld, s_io, s_tr, s_ev, s_r = p.sem("loaded"), p.sem("iota"), p.sem("transposed"), p.sem("evacuated"), p.sem("rows")
    block = Bodies()

    @block.sync
    def _(e):
        e.dma_start(t.dsti, d["dst_pt"][:, 0:EDGE_TILES]).then_inc(s_ld, 16)
        e.dma_start(t.rels, d["typ_pt"][:, 0:EDGE_TILES]).then_inc(s_ld, 16)
        e.dma_start(t.gbase, d["gbase"].partition_broadcast(P)).then_inc(s_ld, 16)
        e.dma_start(t.idx, d["src_pt"][:, 0:EDGE_TILES]).then_inc(s_ld, 16)
        e.dma_start(t.edge2[:, 1, :], d["w_pt"][:, 0:EDGE_TILES]).then_inc(s_ld, 16)
        e.dma_start(t.hrows, d["rows_0"].rearrange("(b p) f -> p b f", p=P)).then_inc(s_r, 16)
        e.wait_ge(s_ld, 5 * 16)
        e.wait_ge(s_r, 16)

    @block.gpsimd
    def _(e):
        e.iota(t.iota, [[1, REL * WIN]], base=0, channel_multiplier=0,
               allow_small_or_imprecise_dtypes=True).then_inc(s_io, 1)

    @block.vector
    def _(e):
        v = Tally(p.sem("setup"))
        e.wait_ge(s_ld, 5 * 16)
        v.inc(e.tensor_copy(t.typf, t.rels))
        v.inc(e.tensor_copy(t.dstf, t.dsti))
        v.link(e, e.tensor_copy(t.gbf, t.gbase))
        v.link(e, e.tensor_tensor(t.dstf.rearrange("p (g k) -> p g k", k=GT),
                                  t.dstf.rearrange("p (g k) -> p g k", k=GT),
                                  bcast(t.gbf[:, 0:EDGE_TILES // GT], P, GT, EDGE_TILES // GT), ALU.subtract))
        v.inc(e.scalar_tensor_tensor(t.edge2[:, 0, :], t.typf, float(WIN), t.dstf, ALU.mult, ALU.add))
        e.wait_ge(s_io, 1)
        for g in range(7):
            n = min(4, BLOCKS - 4 * g)
            e.wait_ge(s_tr, g + 1)
            e.tensor_copy(t.ht[:, g * 512:g * 512 + n * P], p.psum[:, g, 0:n * P]).then_inc(s_ev, 1)

    @block.tensor
    def _(e):
        e.wait_ge(s_r, 16)
        for b in range(BLOCKS):
            m = e.transpose(p.psum[:, b // 4, (b % 4) * P:(b % 4 + 1) * P], t.hrows[:, b, :], p.ident[:, :])
            if b % 4 == 3 or b == BLOCKS - 1:
                m.then_inc(s_tr, 1)
    return block


def general_relations(p, t, l):
    y = p.psum[:, 2:6, :].rearrange("p a (c o) -> p (a c) o", o=RF)
    by_o = t.gen_y.rearrange("p (r o) -> p o r", r=REL)
    steps = [("vector", lambda e, i: e.tensor_copy(t.pick[:, 0:1], t.idx[:, bass.ds(i, 1)])),
             ("gpsimd", lambda e, i: e.indirect_dma_start(
                 out=t.msg[:, 0, :], out_offset=None, in_=p.d[f"rows_{l}"][:, :],
                 in_offset=bass.IndirectOffsetOnAxis(ap=t.pick[:, 0:1], axis=0))),
             ("tensor", lambda e, i: e.transpose(p.psum[:, 1, 0:P], t.msg[:, 0, :], p.ident[:, :])),
             ("vector", lambda e, i: e.tensor_copy(t.msg[:, 1, :], p.psum[:, 1, 0:P]))]
    for q in range(4):
        steps.append(("tensor", lambda e, i, q=q: e.matmul(
            p.psum[:, 2 + q, :], t.msg[:, 1, :], t.wr[:, 4 * q:4 * q + 4, :].rearrange("p r o -> p (r o)"),
            start=True, stop=True)))
    steps += [("vector", lambda e, i: e.tensor_tensor(
                  t.gen_rel, t.iota[:, 0:REL], t.gen_types[:, bass.ds(i, 1)].to_broadcast([P, REL]), ALU.is_equal)),
              ("vector", lambda e, i: e.tensor_tensor(
                  t.gen_rel, t.gen_rel, t.edge2[:, 1, bass.ds(i, 1)].to_broadcast([P, REL]), ALU.mult)),
              ("vector", lambda e, i: e.tensor_tensor(
                  t.gen_y.rearrange("p (r o) -> p r o", r=REL), y, bcast(t.gen_rel, P, RF, REL), ALU.mult)),
              ("vector", lambda e, i: e.tensor_reduce(t.msg[:, 2, :], by_o, AX.X, ALU.add)),
              place_of_dst(t, lambda i: t.gen_to[:, bass.ds(i, 1)])]
    for k in range(NW):
        at = t.acc[:, k * GW:(k + 1) * GW]
        steps += [one_hot_of_dst(t, k),
                  ("tensor", lambda e, i: e.matmul(p.psum[:, 0, 0:GW], t.msg[:, 2, :], t.gen_oh, start=True, stop=True)),
                  ("vector", lambda e, i, at=at: e.tensor_tensor(at, at, p.psum[:, 0, 0:GW], ALU.add))]
    return Serial(p, steps, EDGE_TILES)


def relation_layer(p, t, l, fast):
    nc, d = p.nc, p.d
    PER = ROUND
    G = PER // GT
    FULL = EDGE_TILES // PER
    REST = EDGE_TILES - FULL * PER
    last = l == 2
    s_ld, s_x1, s_rt, s_ac, s_pk, s_oh, s_ag, s_ev, s_ot, s_ad, s_fr = (p.sem(n) for n in (
        "weights", "x1", "root", "root_added", "picked", "onehots", "means", "evacuated", "outputs", "added", "freed"))
    s_hr, s_so = p.sem("by_nodes"), p.sem("stored")
    s_got = [p.sem(f"rows{k}") for k in range(PER)]
    passed = p.sem("passed")
    loop = None
    if not fast:
        loop, s_go = general_relations(p, t, l), p.sem("constants")
    MEAN, OUT = 0, 4
    block = Bodies()

    @block.sync
    def _(e):
        e.dma_start(t.wr, d["W"][l].rearrange("r f o -> f r o")).then_inc(s_ld, 16)
        e.dma_start(t.root, d["root"][l]).then_inc(s_ld, 16)
        e.dma_start(t.bias, d["bias"][l].rearrange("(o b) -> o b", b=1)).then_inc(s_ld, 16)
        e.wait_ge(s_ld, 48)
        if last:
            e.dma_start(t.x1, d["x1"].rearrange("(b p) f -> p b f", p=P)).then_inc(s_x1, 16)
            e.wait_ge(s_x1, 16)
        to = d["out"] if last else d[f"rows_{l + 1}"]
        parts = [(g, 4 * g, min(BLOCKS, 4 * g + 4)) for g in range(7)]
        whole = BLOCKS - 1 if last else BLOCKS
        for g, b0, b1 in parts:
            e.wait_ge(s_hr, g + 1)
            if b0 < whole:
                e.dma_start(to[b0 * P:b1 * P, :].rearrange("(b p) f -> p b f", p=P),
                            t.hrows[:, b0:b1, :]).then_inc(s_so, 16)
            else:
                e.dma_start(to[b0 * P:NODES, :], t.hrows[0:NODES - b0 * P, b0, :]).then_inc(s_so, 16)
        e.wait_ge(s_so, 16 * len(parts))

    @block.gpsimd
    def _(e):
        if not fast:
            big = dict(allow_small_or_imprecise_dtypes=True)
            e.iota(t.gen_iota, [[1, GW]], base=0, channel_multiplier=0, **big).then_inc(s_go, 1)
            e.iota(t.gen_starts, [[GW, NW]], base=0, channel_multiplier=0, **big).then_inc(s_go, 1)
            loop.body(e, "gpsimd")
            return

        def gather(i, k):
            held(e, s_pk, i * PER + k + 1, passed)
            e.indirect_dma_start(out=t.msg[:, k, :], out_offset=None, in_=d[f"rows_{l}"][:, :],
                                 in_offset=bass.IndirectOffsetOnAxis(ap=t.pick[:, k:k + 1], axis=0)
                                 ).then_inc(s_got[k], 16)
        with e.Fori(0, FULL) as i:
            for k in range(PER):
                gather(i, k)
        for k in range(REST):
            gather(FULL, k)

    def scalar(e):
        e.sem_inc(s_ev, G)

        def pick(i, k):
            e.activation(t.pick[:, k:k + 1], t.idx[:, bass.ds(i * PER + k, 1)], ACT.Copy).then_inc(s_pk, 1)

        def take(i, g):
            held(e, s_ag, i * PER + (g + 1) * GT + PER, passed)
            if g == 0:
                held(e, s_ot, i + 1, passed)
            e.activation(t.agg[:, :, g, :], p.psum[:, MEAN + g, 0:REL * WIN].rearrange("p (r w) -> p r w", r=REL),
                         ACT.Copy).then_inc(s_ev, 1)

        def turn(i, picks, takes):
            for k in range(takes * GT):
                if k < picks:
                    held(e, s_ag, i * PER + k + 1 + PER, passed)
                    pick(i + 1, k)
                if k % GT == GT - 1:
                    take(i, k // GT)

        for k in range(PER):
            pick(0, k)
        with e.Fori(0, FULL - 1) as i:
            turn(i, PER, G)
        turn(FULL - 1, REST, G)
        turn(FULL, 0, REST // GT)

    if fast:
        block.scalar(scalar)

    @block.vector
    def _(e):
        v = Tally(p.sem("out_adds"))
        regs = [e.alloc_register(f"out_base{l}_{int(fast)}_{k}") for k in range(G)]
        e.wait_ge(s_ld, 48)
        for g in range(7):
            n = min(512, NPAD - 512 * g)
            e.wait_ge(s_rt, g + 1)
            v.inc(e.tensor_scalar(t.acc[:, g * 512:g * 512 + n], p.psum[:, g, 0:n], t.bias[:, 0:1], None, ALU.add))
        e.wait_ge(v.sem, v.n)
        e.sem_inc(s_ac)

        def stage(i, n):
            e.wait_ge(s_oh, i * PER + 1)
            v.link(e, e.tensor_copy(t.stage.rearrange("p (a t) -> p a t", a=2)[:, :, 0:n],
                                    t.edge2[:, :, bass.ds(i * PER, n)]))

        def onehots(i, k0, k1):
            for k in range(k0, k1):
                e.wait_ge(s_ag, i * PER + k + 1)
                e.tensor_scalar(t.oh[:, k, :], t.iota, t.stage[:, k:k + 1], t.stage[:, PER + k:PER + k + 1],
                                ALU.is_equal, ALU.mult).then_inc(s_oh, 1)

        def adds(i, groups):
            e.load(regs[0:groups], t.gbase[0:1, bass.ds(i * G, groups)])
            e.wait_ge(s_ot, i + 2)
            for g in range(groups):
                base = e.snap(regs[g], min_val=0, max_val=NODES - 1)
                at = t.acc[:, bass.ds(base, WIN)]
                v.link(e, e.tensor_tensor(at, at, p.psum[:, OUT, g * WIN:(g + 1) * WIN], ALU.add))
            e.sem_inc(s_ad)

        if fast:
            e.sem_inc(s_oh)
            stage(0, PER)
            onehots(0, 0, PER)
            with e.Fori(0, FULL - 1) as i:
                v.enter(i, 1 + G)
                stage(i + 1, PER)
                onehots(i + 1, 0, PER // 2)
                adds(i, G)
                onehots(i + 1, PER // 2, PER)
                v.leave(FULL - 1)
            stage(FULL, REST)
            onehots(FULL, 0, REST)
            adds(FULL - 1, G)
            adds(FULL, REST // GT)
        else:
            e.wait_ge(s_go, 2)
            v.inc(e.tensor_copy(t.gen_types, t.typf))
            v.link(e, e.tensor_copy(t.gen_to, t.dsti))
            loop.body(e, "vector")
        if not last:
            v.link(e, e.tensor_scalar(t.ht, t.acc, 0.0, None, ALU.max))
        e.sem_inc(s_fr)
        for g in range(7):
            n = min(4, BLOCKS - 4 * g)
            e.wait_ge(s_fr, g + 2)
            part = p.psum[:, g, 0:n * P].rearrange("p (b f) -> p b f", b=n)
            if last:
                if g == 0:
                    e.wait_ge(s_x1, 16)
                e.tensor_tensor(t.hrows[:, 4 * g:4 * g + n, :], part, t.x1[:, 4 * g:4 * g + n, :],
                                ALU.add).then_inc(s_hr, 1)
            else:
                e.tensor_copy(t.hrows[:, 4 * g:4 * g + n, :], part).then_inc(s_hr, 1)

    @block.tensor
    def _(e):
        e.wait_ge(s_ld, 48)
        for g in range(7):
            n = min(512, NPAD - 512 * g)
            e.matmul(p.psum[:, g, 0:n], t.root, t.ht[:, g * 512:g * 512 + n], start=True, stop=True).then_inc(s_rt, 1)
        e.wait_ge(s_ac, 1)
        if fast:
            e.sem_inc(s_ag, PER)
            e.sem_inc(s_ot)

            def work(i, groups):
                for g in range(groups):
                    e.wait_ge(s_ev, i * G + g + 1)
                    for k in range(g * GT, g * GT + GT):
                        e.wait_ge(s_got[k], i * 16 + 16)
                        e.wait_ge(s_oh, i * PER + k + 2)
                        e.matmul(p.psum[:, MEAN + g, 0:REL * WIN], t.msg[:, k, :], t.oh[:, k, :],
                                 start=(k % GT == 0), stop=(k % GT == GT - 1)).then_inc(s_ag, 1)
                e.wait_ge(s_ev, i * G + G + groups)
                e.wait_ge(s_ad, i + 1)
                for r in range(REL):
                    m = e.matmul(p.psum[:, OUT, 0:groups * WIN], t.wr[:, r, :],
                                 t.agg[:, r, 0:groups, :].rearrange("p g w -> p (g w)"),
                                 start=(r == 0), stop=(r == REL - 1))
                m.then_inc(s_ot, 1)
            e.sem_inc(s_ad)
            with e.Fori(0, FULL) as i:
                work(i, G)
            work(FULL, REST // GT)
        else:
            loop.body(e, "tensor")
        e.wait_ge(s_fr, 1)
        for b in range(BLOCKS):
            m = e.transpose(p.psum[:, b // 4, (b % 4) * P:(b % 4 + 1) * P],
                            (t.acc if last else t.ht)[:, b * P:(b + 1) * P], p.ident[:, :])
            if b % 4 == 3 or b == BLOCKS - 1:
                m.then_inc(s_fr, 1)
    return block


class Bag:
    pass


def outside(p, t):
    h = p.h16[:, :, :, :].rearrange("p a b c -> p (a b c)").bitcast(F32)
    t.cnt = p.work[0:32, GPAD:GPAD + NPAD]
    at = 2 * TPAD + BLOCKS * WIN // 2 + 4 * AT

    def piece(words, parts=P):
        nonlocal at
        at += words
        return h[0:parts, at - words:at]
    t.rep, t.ident_h = piece(P, 32), piece(P // 2).bitcast(F16)
    t.turned = [piece(16 * 32 // 2).bitcast(F16) for _ in range(2)]
    t.picked = [piece(16 * WIN) for _ in range(2)]
    t.now_r = [piece(CHUNK * 32 // 2).bitcast(F16) for _ in range(2)]
    t.now_c = [piece(CHUNK * WIN // 2).bitcast(F16) for _ in range(2)]
    assert at <= BLOCKS * HID, at


def edge_columns(p):
    t = Bag()
    adjacency_memory(p, t)
    outside(p, t)
    c = p.carve(0)
    t.typf, t.dstf, t.shif, t.dloc, t.wgt = (c(TPAD) for _ in range(5))
    t.src, t.dst, t.typ, t.shi, t.slo = (c(TPAD, I32) for _ in range(5))
    t.gbf, t.gdiff = c(GPAD), c(GPAD)
    t.iota_f = c(REL * WIN)
    t.sig, t.red, t.bad, t.ones, t.deg = c(4), c(10), c(8), c(1), c(BLOCKS)
    t.degr, t.degt = c(BLOCKS), c(BLOCKS)
    t.cnt4 = c(GT * NPAD // 2, F16).rearrange("p (k n) -> p k n", k=GT)
    t.gen_oh, t.gen_iota, t.gen_dst, t.gen_starts = c(GW), c(GW), c(NW), c(NW)
    t.gen_rel, t.gen_relt, t.gen_part, t.gen_sum = c(32), c(P, parts=32), c(NW), c(1)
    before = p.at
    t.gains = c(6 * HID).rearrange("p (k o) -> p k o", k=6)
    c = p.carve(before)
    t.all_r, t.all_c = c(TPAD * 32 // 2, F16), c(TPAD * WIN // 2, F16)
    return t


def scratch(nc, dram):
    def make(name, shape, dt):
        dram[name] = nc.dram_tensor(name, shape, dt).ap()
    make("w_pt", (P, TPAD), F32)
    make("x_pad", (NPAD, RF), F32)
    make("x1", (NPAD, RF), F32)
    for l in range(4):
        make(f"h16_{l}", (NPAD, 2, RF if l == 0 else HID), F16)
    for l in range(3):
        make(f"rows_{l}", (NPAD, RF), F32)


def build(nc, dram):
    with ExitStack() as ctx:
        p = Prog(nc, ctx, dram)
        scratch(nc, dram)
        t = edge_columns(p)
        run(p, prepare(p, t))
        run(p, count_relations(p, t), count_relations_general(p, t))
        run(p, edge_weights(p, t), edge_weights_general(p, t))
        run(p, first_norm(p, norm_memory(p), True), first_norm(p, norm_memory(p), False))
        run(p, build_adjacency(p, t), Bodies())
        run(p, gcn_layers(p, True), gcn_layers(p, False))
        t = relation_memory(p)
        run(p, relation_setup(p, t))
        for l in range(3):
            run(p, relation_layer(p, t, l, True), relation_layer(p, t, l, False))
_F32 = ["x", "g0", "g1", "g2", "beta0", "beta1", "beta2", "b0", "b1", "b2", "b3", "a0", "a1", "a2",
        "W0", "W1", "W2", "W3"]


def kernel(**inputs):
    import concourse.bacc as bacc
    from concourse.bass_utils import run_bass_kernel_spmd as run
    nc = bacc.Bacc("TRN2", target_bir_lowering=False, num_devices=1)
    given = {n: np.ascontiguousarray(inputs["x" if n == "x" else f"L0_gnn_{n}"]) for n in _F32}
    given["W"], given["root"], given["bias"] = (np.ascontiguousarray(inputs[f"L1_gnn_{n}"]) for n in ("W", "root", "bias"))

    def tiles(a, fill):
        flat = np.full(TPAD * P, fill, np.int32)
        flat[:EDGES] = a
        return flat

    src, dst, typ = tiles(inputs["src"], 0), tiles(inputs["dst"], -1), tiles(inputs["edge_type_16"], 0)
    for name, a in (("src", src), ("dst", dst), ("typ", typ)):
        given[name + "_pt"] = np.ascontiguousarray(a.reshape(TPAD, P).T)
    gbase = dst[::GT * P].copy()
    gbase[-(-TILES // GT):] = 0
    given["gbase"] = gbase
    dram = {}
    for n, a in given.items():
        dram[n] = nc.dram_tensor("in_" + n, a.shape, mybir.dt.from_np(a.dtype), kind="ExternalInput").ap()
    dram["out"] = nc.dram_tensor("out", (NODES, RF), F32, kind="ExternalOutput").ap()
    build(nc, dram)
    r = run(nc, [{"in_" + n: a for n, a in given.items()}], core_ids=[0])
    return r.results[0]["out"]
```
